# Optimizing a Trainium2 kernel written in Bass

```python
import numpy as np
import jax
import jax.numpy as jnp

def _softmax(x, axis=-1):
    return jax.nn.softmax(x, axis=axis)

def _gelu(x):
    return jax.nn.gelu(x, approximate=True)

def _silu(x):
    return jax.nn.silu(x)

def _sigmoid(x):
    return jax.nn.sigmoid(x)

def _layernorm(x, axis=-1, eps=1e-05):
    m = jnp.mean(x, axis=axis, keepdims=True)
    v = jnp.var(x, axis=axis, keepdims=True)
    return (x - m) / jnp.sqrt(v + eps)

def _scatter_add(tgt, idx, src, axis=0):
    return tgt.at[idx].add(src)

def _segment_sum(src, seg, n):
    return jax.ops.segment_sum(src, seg, n)
kernel_name = 'mk_macaron_d1_jaxref_r4_5ff95c'

def setup_inputs(seed: int=0):
    np.random.seed(seed)
    _w = jnp.asarray

    def _L0_attn_setup():
        import jax, jax.numpy as jnp
        import numpy as np
        CHUNK = 32
        key = jax.random.key(seed)
        ks = jax.random.split(key, 7)
        B, T, D = (4, 2048, 256)
        s = 1.0 / np.sqrt(D)
        return {'x': jax.random.normal(ks[0], (B, T, D), jnp.float32), 'W_q': jax.random.normal(ks[1], (D, D), jnp.float32) * s, 'W_k': jax.random.normal(ks[2], (D, D), jnp.float32) * s, 'W_v': jax.random.normal(ks[3], (D, D), jnp.float32) * s, 'W_g': jax.random.normal(ks[4], (D, D), jnp.float32) * s, 'W_o': jax.random.normal(ks[5], (D, D), jnp.float32) * s, 'log_decay': jax.random.normal(ks[6], (D,), jnp.float32) * 0.1}
    _L0_attn_in = _L0_attn_setup()

    def _L0_ffn_setup():
        import jax, jax.numpy as jnp
        import numpy as np
        B, N, D = (4, 1024, 256)
        E, S, F = (16, 64, 512)
        DO = 256
        EPS = 1e-05

        def _layernorm(x, g, b):
            mu = jnp.mean(x, axis=-1, keepdims=True)
            var = jnp.mean(jnp.square(x - mu), axis=-1, keepdims=True)
            return (x - mu) * jax.lax.rsqrt(var + EPS) * g + b
        key = jax.random.key(seed)
        ks = jax.random.split(key, 8)
        d = {'x': jax.random.normal(ks[0], (B, N, D), dtype=jnp.float32), 'norm_g': jnp.ones((D,), jnp.float32), 'norm_b': jnp.zeros((D,), jnp.float32), 'slot_g': jnp.ones((D,), jnp.float32), 'slot_b': jnp.zeros((D,), jnp.float32), 'scale': jnp.ones((1,), jnp.float32), 'slot_embeds': jax.random.normal(ks[1], (E, S, D), jnp.float32) / np.sqrt(D), 'Wg': jax.random.normal(ks[2], (E, D, F), jnp.float32) * np.sqrt(2.0 / (D + F)), 'bg': jnp.zeros((E, F), jnp.float32), 'Wu': jax.random.normal(ks[3], (E, D, F), jnp.float32) * np.sqrt(2.0 / (D + F)), 'bu': jnp.zeros((E, F), jnp.float32), 'Wd': jax.random.normal(ks[4], (E, F, DO), jnp.float32) * np.sqrt(2.0 / (F + DO)), 'bd': jnp.zeros((E, DO), jnp.float32)}
        return d
    _L0_ffn_in = _L0_ffn_setup()
    _d = {'L0_attn_x': _L0_attn_in['x'], 'L0_attn_W_q': _L0_attn_in['W_q'], 'L0_attn_W_k': _L0_attn_in['W_k'], 'L0_attn_W_v': _L0_attn_in['W_v'], 'L0_attn_W_g': _L0_attn_in['W_g'], 'L0_attn_W_o': _L0_attn_in['W_o'], 'L0_attn_log_decay': _L0_attn_in['log_decay'], 'L0_ffn_norm_g': _L0_ffn_in['norm_g'], 'L0_ffn_norm_b': _L0_ffn_in['norm_b'], 'L0_ffn_slot_g': _L0_ffn_in['slot_g'], 'L0_ffn_slot_b': _L0_ffn_in['slot_b'], 'L0_ffn_scale': _L0_ffn_in['scale'], 'L0_ffn_slot_embeds': _L0_ffn_in['slot_embeds'], 'L0_ffn_Wg': _L0_ffn_in['Wg'], 'L0_ffn_bg': _L0_ffn_in['bg'], 'L0_ffn_Wu': _L0_ffn_in['Wu'], 'L0_ffn_bu': _L0_ffn_in['bu'], 'L0_ffn_Wd': _L0_ffn_in['Wd'], 'L0_ffn_bd': _L0_ffn_in['bd']}
    _x0 = _d['L0_attn_x']
    _d['L0_attn_x'] = jax.random.normal(jax.random.fold_in(jax.random.key(seed), 1), (4, 2048, 256), dtype=_x0.dtype)
    del _x0
    return _d

def reference(L0_attn_x, L0_attn_W_q, L0_attn_W_k, L0_attn_W_v, L0_attn_W_g, L0_attn_W_o, L0_attn_log_decay, L0_ffn_norm_g, L0_ffn_norm_b, L0_ffn_slot_g, L0_ffn_slot_b, L0_ffn_scale, L0_ffn_slot_embeds, L0_ffn_Wg, L0_ffn_bg, L0_ffn_Wu, L0_ffn_bu, L0_ffn_Wd, L0_ffn_bd):

    def _L0_attn_ref(x, W_q, W_k, W_v, W_g, W_o, log_decay):
        import jax, jax.numpy as jnp
        import numpy as np
        CHUNK = 32
        B, T, D = x.shape
        C = CHUNK
        nc = T // C
        Q = x @ W_q.T
        K = x @ W_k.T
        V = x @ W_v.T
        decay = jax.lax.stop_gradient(jax.nn.sigmoid(log_decay[0]))
        pos = jnp.arange(C, dtype=x.dtype)
        diff = pos[:, None] - pos[None, :]
        mask = jnp.where(diff >= 0, decay ** diff, jnp.zeros((), x.dtype))
        Qc = Q.reshape(B, nc, C, D)
        Kc = K.reshape(B, nc, C, D)
        Vc = V.reshape(B, nc, C, D)
        S = jnp.einsum('bncd,bnkd->bnck', Qc, Kc) * mask
        O = jnp.einsum('bnck,bnkd->bncd', S, Vc).reshape(B, T, D)
        gate = jax.nn.sigmoid(x @ W_g.T)
        out = gate * O @ W_o.T + x
        return out

    def _L0_ffn_ref(x, norm_g, norm_b, slot_g, slot_b, scale, slot_embeds, Wg, bg, Wu, bu, Wd, bd):
        import jax, jax.numpy as jnp
        import numpy as np
        B, N, D = (4, 1024, 256)
        E, S, F = (16, 64, 512)
        DO = 256
        EPS = 1e-05

        def _layernorm(x, g, b):
            mu = jnp.mean(x, axis=-1, keepdims=True)
            var = jnp.mean(jnp.square(x - mu), axis=-1, keepdims=True)
            return (x - mu) * jax.lax.rsqrt(var + EPS) * g + b
        x = _layernorm(x, norm_g, norm_b)
        se = _layernorm(slot_embeds, slot_g, slot_b) * scale
        logits = jnp.einsum('bnd,esd->bnes', x, se)
        dispatch = jax.nn.softmax(logits, axis=1)
        combine = jax.nn.softmax(logits.reshape(x.shape[0], x.shape[1], -1), axis=-1)
        slots = jnp.einsum('bnd,bnes->besd', x, dispatch)
        gate = jax.nn.gelu(jnp.einsum('besd,edf->besf', slots, Wg) + bg[None, :, None, :], approximate=False)
        up = jnp.einsum('besd,edf->besf', slots, Wu) + bu[None, :, None, :]
        eout = jnp.einsum('besf,efo->beso', gate * up, Wd) + bd[None, :, None, :]
        eout = eout.reshape(eout.shape[0], -1, eout.shape[-1])
        return jnp.einsum('bns,bso->bno', combine, eout)
    x = L0_attn_x
    x = x + 0.5 * _L0_ffn_ref(_layernorm(x, axis=-1), L0_ffn_norm_g, L0_ffn_norm_b, L0_ffn_slot_g, L0_ffn_slot_b, L0_ffn_scale, L0_ffn_slot_embeds, L0_ffn_Wg, L0_ffn_bg, L0_ffn_Wu, L0_ffn_bu, L0_ffn_Wd, L0_ffn_bd)
    x = x + _L0_attn_ref(_layernorm(x, axis=-1), L0_attn_W_q, L0_attn_W_k, L0_attn_W_v, L0_attn_W_g, L0_attn_W_o, L0_attn_log_decay)
    x = x + 0.5 * _L0_ffn_ref(_layernorm(x, axis=-1), L0_ffn_norm_g, L0_ffn_norm_b, L0_ffn_slot_g, L0_ffn_slot_b, L0_ffn_scale, L0_ffn_slot_embeds, L0_ffn_Wg, L0_ffn_bg, L0_ffn_Wu, L0_ffn_bu, L0_ffn_Wd, L0_ffn_bd)
    return x

_drawn_inputs = setup_inputs


def setup_inputs(seed=0):
    import zlib

    import numpy as np

    out = dict(_drawn_inputs(seed))
    spreads = {'L0_ffn_norm_g': (1.0, 0.2),
     'L0_ffn_norm_b': (0.0, 0.1),
     'L0_ffn_slot_g': (1.0, 0.2),
     'L0_ffn_slot_b': (0.0, 0.1),
     'L0_ffn_bg': (0.0, 0.1),
     'L0_ffn_bu': (0.0, 0.1),
     'L0_ffn_bd': (0.0, 0.1)}
    factors = {}
    for name, (base, spread) in spreads.items():
        noise = np.random.default_rng([zlib.crc32(name.encode()), seed]).standard_normal(out[name].shape)
        drawn = base * np.exp(spread * noise) if base else spread * noise
        out[name] = jnp.asarray(drawn.astype(out[name].dtype))
    for name, factor in factors.items():
        out[name] = (out[name] * factor).astype(out[name].dtype)
    return out
```

```python
from contextlib import ExitStack

import concourse.bass as bass
from concourse import mybir

F32 = mybir.dt.float32
F32R = mybir.dt.float32r
ALU = mybir.AluOpType
ACT = mybir.ActivationFunctionType
AX_X = mybir.AxisListType.X

P = 128
B, T, D = 4, 2048, 256
E, S, F = 16, 64, 512
CHUNK = 32
EPS = 1e-5
KD = D // P
KF = F // P
SL = E * S
NSC = SL // P
GT = 4
GN = GT * P
NG = T // GN
BANK = 512
HB = SL // BANK
DMA = 16


class Scope:

    def __init__(self, nc, ctx, tag):
        self.nc, self.ctx, self.tag, self.sems = nc, ctx, tag, []
        ctx.callback(self.release)

    def sb(self, name, shape, dt=F32):
        return self.ctx.enter_context(self.nc.sbuf_tensor(self.tag + name, shape, dt))

    def ps(self, name, shape):
        return self.ctx.enter_context(self.nc.psum_tensor(self.tag + name, shape, F32))

    def sem(self, name):
        self.sems.append(self.nc.alloc_semaphore(self.tag + name))
        return self.sems[-1]

    def release(self):
        if self.sems:
            self.nc.clear_and_free_semaphores(self.sems)
            self.nc.all_engine_barrier()


def rd(ap):
    return ap.bitcast(F32)


def dve_wait(dve, c, sem, value):
    dve.wait_ge(sem, value)
    dve.memset(c["dve_carrier"][:, :], 0.0)


def pool_wait(pool, c, sem, value):
    pool.wait_ge(sem, value)
    pool.tensor_tensor(c["pool_carrier"][:, :], c["minus_half"][:, 0:1], c["minus_half"][:, 0:1], ALU.add)


def setup_stage(nc, c, prm):
    with ExitStack() as ctx:
        al = Scope(nc, ctx, "su_")
        emb = al.sb("emb", [P, NSC, D])
        slot_g, slot_b, scale = al.sb("slot_g", [P, D]), al.sb("slot_b", [P, D]), al.sb("scale", [P, 1])
        bias_rows = al.sb("bias_rows", [E * KF, 2, P])
        stats, mv = al.sb("stats", [P, NSC, 6]), al.sb("mv", [P, NSC, 2])
        var_eps, rstd = al.sb("var_eps", [P, NSC]), al.sb("rstd", [P, NSC])
        tr = [al.ps(f"tr{i}", [P, BANK]) for i in range(2)]
        loads, const_done, ident_zero = al.sem("loads"), al.sem("const_done"), al.sem("ident_zero")
        stats_done, mv_done, var_done = al.sem("stats_done"), al.sem("mv_done"), al.sem("var_done")
        rstd_done, emb_step, emb_done = al.sem("rstd_done"), al.sem("emb_step"), al.sem("emb_done")
        tr_done, hi_done, lo_done = al.sem("tr_done"), al.sem("hi_done"), al.sem("lo_done")
        bias_tr, bias_done = al.sem("bias_tr"), al.sem("bias_done")
        block = ctx.enter_context(nc.Block())

        def row(v):
            return v.rearrange("(a n) -> a n", a=1).to_broadcast([P, v.shape[0]])

        @block.sync
        def _(sp):
            sp.dma_start(emb[:, :, :], prm["slot_embeds"].rearrange("e s d -> (e s) d")
                         .rearrange("(t p) d -> p t d", p=P)).then_inc(loads, DMA)
            sp.dma_start(slot_g[:, :], row(prm["slot_g"])).then_inc(loads, DMA)
            sp.dma_start(slot_b[:, :], row(prm["slot_b"])).then_inc(loads, DMA)
            sp.dma_start(scale[:, :], row(prm["scale"])).then_inc(loads, DMA)
            sp.dma_start(c["norm_g"][:, :], row(prm["norm_g"])).then_inc(loads, DMA)
            sp.dma_start(c["norm_b"][:, :], row(prm["norm_b"])).then_inc(loads, DMA)
            for i, name in enumerate(("bg", "bu")):
                sp.dma_start(bias_rows[:, i, :], prm[name].rearrange("e (c p) -> (e c) p", p=P)).then_inc(loads, DMA)
            sp.wait_ge(loads, 8 * DMA)

        @block.gpsimd
        def _(pool):
            pool.memset(c["ones"][:, :], 1.0).then_inc(const_done, 1)
            pool.memset(c["minus_half"][:, :], -0.5).then_inc(const_done, 1)
            pool.memset(c["ident"][:, :], 0.0).then_inc(ident_zero, 1)
            pool.wait_ge(ident_zero, 1)
            pool.affine_select(out=c["ident"][:, :], in_=c["ident"][:, :], compare_op=ALU.not_equal, fill=1.0,
                               base=0, pattern=[[-1, P]], channel_multiplier=1).then_inc(const_done, 1)
            pool.wait_ge(mv_done, NSC)
            pool.tensor_scalar(var_eps[:, :], mv[:, :, 1], 1.0, EPS, ALU.mult, ALU.add).then_inc(var_done, 1)
            pool.wait_ge(var_done, 1)
            pool.wait_ge(const_done, 3)
            pool.tensor_tensor(rstd[:, :], var_eps[:, :], c["minus_half"][:, 0:NSC], ALU.pow).then_inc(rstd_done, 1)

        @block.vector
        def _(dve):
            dve.wait_ge(loads, 8 * DMA)
            for t in range(NSC):
                dve.bn_stats(stats[:, t, :], emb[:, t, :]).then_inc(stats_done, 1)
            for t in range(NSC):
                dve.wait_ge(stats_done, t + 1)
                dve.bn_aggr(mv[:, t, :], stats[:, t, :]).then_inc(mv_done, 1)
            dve.wait_ge(rstd_done, 1)
            dve.wait_ge(mv_done, NSC)
            for t in range(NSC):
                dve.tensor_scalar(emb[:, t, :], emb[:, t, :], mv[:, t, 0:1], rstd[:, t:t + 1],
                                  ALU.subtract, ALU.mult).then_inc(emb_step, 1)
            dve.wait_ge(emb_step, NSC)
            dve.tensor_tensor(emb[:, :, :], emb[:, :, :], slot_g[:, :].unsqueeze(1).to_broadcast([P, NSC, D]),
                              ALU.mult).then_inc(emb_step, 1)
            dve.wait_ge(emb_step, NSC + 1)
            dve.tensor_tensor(emb[:, :, :], emb[:, :, :], slot_b[:, :].unsqueeze(1).to_broadcast([P, NSC, D]),
                              ALU.add).then_inc(emb_step, 1)
            dve.wait_ge(emb_step, NSC + 2)
            dve.tensor_scalar(emb[:, :, :], emb[:, :, :], scale[:, 0:1], None, ALU.mult).then_inc(emb_done, 1)
            for n in range(KD * HB):
                k, h = n // HB, n % HB
                dve.wait_ge(hi_done, n + 1)
                dve.tensor_tensor(c["emb_lo"][:, k, h * BANK:(h + 1) * BANK], tr[n % 2][:, :],
                                  rd(c["emb_hi"][:, k, h * BANK:(h + 1) * BANK]), ALU.subtract).then_inc(lo_done, 1)

        @block.tensor
        def _(pe):
            pe.wait_ge(const_done, 3)
            pe.wait_ge(emb_done, 1)
            for n in range(KD * HB):
                k, h = n // HB, n % HB
                if n >= 2:
                    pe.wait_ge(lo_done, n - 1)
                for j in range(BANK // P):
                    mm = pe.transpose(tr[n % 2][:, j * P:(j + 1) * P], emb[:, h * (BANK // P) + j, k * P:(k + 1) * P],
                                      c["ident"][:, :])
                mm.then_inc(tr_done, 1)
            pe.wait_ge(lo_done, KD * HB)
            for i in range(2):
                mm = pe.transpose(tr[0][:, i * E * KF:(i + 1) * E * KF], bias_rows[:, i, :],
                                  c["ident"][0:E * KF, 0:E * KF])
            mm.then_inc(bias_tr, 1)

        @block.scalar
        def _(act):
            for n in range(KD * HB):
                k, h = n // HB, n % HB
                act.wait_ge(tr_done, n + 1)
                act.activation(c["emb_hi"][:, k, h * BANK:(h + 1) * BANK], tr[n % 2][:, :], ACT.Copy).then_inc(hi_done, 1)
            act.wait_ge(bias_tr, 1)
            act.activation(c["biases"][:, :], tr[0][:, 0:2 * E * KF], ACT.Copy).then_inc(bias_done, 1)


def route_stage(nc, c, tag, x_in, slots, logits_dram, xhat_dram):
    with ExitStack() as ctx:
        al = Scope(nc, ctx, tag)
        lt = al.sb("lt", [P, NG, NSC, GN])
        et = al.sb("et", [P, NSC, GN])
        xin = [al.sb(f"xin{i}", [P, GT, D]) for i in range(2)]
        xhat = [al.sb(f"xhat{i}", [P, GT, D]) for i in range(2)]
        xT_hi = [al.sb(f"xT_hi{i}", [P, KD, GN], F32R) for i in range(2)]
        xT_lo = [al.sb(f"xT_lo{i}", [P, KD, GN], F32R) for i in range(2)]
        xback = [al.sb(f"xback{i}", [P, GT, D]) for i in range(2)]
        xs_hi = [al.sb(f"xs_hi{i}", [P, D], F32R) for i in range(2)]
        xs_lo = [al.sb(f"xs_lo{i}", [P, D], F32R) for i in range(2)]
        e_hi = [al.sb(f"e_hi{i}", [P, SL], F32R) for i in range(2)]
        e_lo = [al.sb(f"e_lo{i}", [P, SL], F32R) for i in range(2)]
        diag, inv_rows = al.sb("diag", [P, NSC, P]), al.sb("inv_rows", [P, SL])
        stats, mv = al.sb("stats", [P, GT, 6]), [al.sb(f"mv{i}", [P, GT, 2]) for i in range(2)]
        var_eps, rstd = al.sb("var_eps", [P, GT]), [al.sb(f"rstd{i}", [P, GT]) for i in range(2)]
        gmax, neg_max = al.sb("gmax", [P, NSC, NG]), al.sb("neg_max", [P, NSC])
        gsum, tsum, inv = al.sb("gsum", [P, NSC, NG]), al.sb("tsum", [P, NSC]), al.sb("inv", [P, NSC])

        ps_l = [al.ps(f"ps_l{i}", [P, BANK]) for i in range(2)]
        ps_t = [al.ps(f"ps_t{i}", [P, BANK]) for i in range(HB)]
        ps_s = [al.ps(f"ps_s{i}", [P, BANK]) for i in range(KD * HB)]

        x_loaded = [al.sem(f"x_loaded{i}") for i in range(2)]
        xhat_stored = [al.sem(f"xhat_stored{i}") for i in range(2)]
        xback_loaded = [al.sem(f"xback_loaded{i}") for i in range(2)]
        lt_stored = [al.sem(f"lt_stored{g}") for g in range(NG)]
        stats_done, mv_done, var_done, rstd_done = (al.sem(n) for n in ("stats_done", "mv_done", "var_done", "rstd_done"))
        xn_done, gain_done, xhat_done = (al.sem(n) for n in ("xn_done", "gain_done", "xhat_done"))
        xT_tr, xT_hi_done, xT_lo_done = (al.sem(n) for n in ("xT_tr", "xT_hi_done", "xT_lo_done"))
        logit_mm, logit_out, max_done = (al.sem(n) for n in ("logit_mm", "logit_out", "max_done"))
        exp_done, e_tr, e_hi_done, e_lo_done = (al.sem(n) for n in ("exp_done", "e_tr", "e_hi_done", "e_lo_done"))
        xs_hi_done, xs_done, dispatched = (al.sem(n) for n in ("xs_hi_done", "xs_done", "dispatched"))
        tsum_done, inv_done, diag_done = (al.sem(n) for n in ("tsum_done", "inv_done", "diag_done"))
        inv_mm, inv_out, slots_done = (al.sem(n) for n in ("inv_mm", "inv_out", "slots_done"))
        block = ctx.enter_context(nc.Block())

        LAST = B * NG - 1

        def batches(eng, emit):
            emit(0, True, False)
            with eng.Fori(1, B - 1) as b:
                emit(b, True, True)
            emit(B - 1, True, True)
            emit(B, False, True)

        def exists(b, g, ahead):
            return not isinstance(b, int) or b * NG + g + ahead <= LAST

        @block.sync
        def _(sp):
            x_g = x_in.rearrange("b (g p t) d -> (b g) p t d", g=NG, t=GT)

            def load_x(b, g, ahead):
                i, par = b * NG + g + ahead, (g + ahead) % 2
                sp.dma_start(xin[par][:, :, :], x_g[i]).then_inc(x_loaded[par], DMA)

            for n in range(3):
                if n == 2:
                    sp.wait_ge(xhat_done, 1)
                load_x(0, 0, n)
            for n in range(2):
                sp.wait_ge(xhat_done, n + 1)
                sp.dma_start(xhat_dram[n], xhat[n][:, :, :]).then_inc(xhat_stored[n], DMA)

            def emit(b, fill, drain):
                for g in range(NG):
                    i = b * NG + g
                    if fill and exists(b, g, 3):
                        sp.wait_ge(xhat_done, i + 2)
                        load_x(b, g, 3)
                    if fill and (drain or g == NG - 1):
                        par = (g + 1) % 2
                        if drain:
                            sp.wait_ge(xs_done, GT * (i - NG))
                        sp.wait_ge(xhat_stored[par], DMA * ((i + 1 - NG) // 2 + 1))
                        sp.dma_start(xback[par][:, :, :], xhat_dram[i + 1 - NG]).then_inc(xback_loaded[par], DMA)
                    elif not fill and g < NG - 1:
                        par = (g + 1) % 2
                        sp.wait_ge(xs_done, GT * (i - NG))
                        sp.wait_ge(xhat_stored[par], DMA * ((i + 1 - NG) // 2 + 1))
                        sp.dma_start(xback[par][:, :, :], xhat_dram[i + 1 - NG]).then_inc(xback_loaded[par], DMA)
                    if fill:
                        sp.wait_ge(logit_out, NSC * (i + 1))
                        sp.dma_start(logits_dram[i], lt[:, g, :, :]).then_inc(lt_stored[g], DMA)
                        if exists(b, g, 2):
                            sp.wait_ge(xhat_done, i + 3)
                            sp.dma_start(xhat_dram[i + 2], xhat[g % 2][:, :, :]).then_inc(xhat_stored[g % 2], DMA)

            batches(sp, emit)
            for s in lt_stored:
                sp.wait_ge(s, B * DMA)
            for s in xhat_stored:
                sp.wait_ge(s, B * NG // 2 * DMA)

        @block.gpsimd
        def _(pool):
            gain = c["norm_g"][:, :].unsqueeze(1).to_broadcast([P, GT, D])
            shift = c["norm_b"][:, :].unsqueeze(1).to_broadcast([P, GT, D])

            def affine(i, par, stored):
                pool_wait(pool, c, mv_done, GT * (i + 1))
                pool.tensor_scalar(var_eps[:, :], mv[par][:, :, 1], 1.0 + EPS, EPS * EPS,
                                   ALU.mult, ALU.add).then_inc(var_done, 1)
                pool.wait_ge(var_done, i + 1)
                pool.tensor_tensor(rstd[par][:, :], var_eps[:, :], c["minus_half"][:, 0:GT],
                                   ALU.pow).then_inc(rstd_done, 1)
                pool.wait_ge(xn_done, i + 1)
                if stored is not None:
                    pool.wait_ge(xT_tr, KD * (i - 1))
                    pool.wait_ge(xhat_stored[par], stored)
                pool.tensor_tensor(xhat[par][:, :, :], xin[par][:, :, :], gain, ALU.mult).then_inc(gain_done, 1)
                pool.wait_ge(gain_done, i + 1)
                pool.tensor_tensor(xhat[par][:, :, :], xhat[par][:, :, :], shift, ALU.add).then_inc(xhat_done, 1)

            affine(0, 0, None)
            affine(1, 1, None)

            def emit(b, fill, drain):
                for g in range(NG):
                    if fill and exists(b, g, 2):
                        affine(b * NG + g + 2, g % 2, DMA * (b * (NG // 2) + g // 2 + 1))

            batches(pool, emit)

        @block.vector
        def _(dve):
            def token_stats(i, par):
                dve.wait_ge(x_loaded[par], DMA * (i // 2 + 1))
                for t in range(GT):
                    dve.bn_stats(stats[:, t, :], xin[par][:, t, :]).then_inc(stats_done, 1)
                dve_wait(dve, c, stats_done, GT * (i + 1))
                for t in range(GT):
                    dve.bn_aggr(mv[par][:, t, :], stats[:, t, :]).then_inc(mv_done, 1)

            def normalize(i, par):
                dve.wait_ge(rstd_done, i + 1)
                dve.wait_ge(mv_done, GT * (i + 1))
                for t in range(GT):
                    last = dve.tensor_scalar(xin[par][:, t, :], xin[par][:, t, :], mv[par][:, t, 0:1],
                                             rstd[par][:, t:t + 1], ALU.subtract, ALU.mult)
                last.then_inc(xn_done, 1)

            def transposed_lo(i, par, k):
                dve.wait_ge(xT_hi_done, KD * i + k + 1)
                dve.tensor_tensor(xT_lo[par][:, k, :], ps_t[k][:, :], rd(xT_hi[par][:, k, :]),
                                  ALU.subtract).then_inc(xT_lo_done, 1)

            def logits_out(b, g, i, sc, drain):
                dve.wait_ge(logit_mm, NSC * i + sc + 1)
                if drain:
                    dve.wait_ge(exp_done, NSC * (i - NG) + sc + 1)
                    dve.wait_ge(lt_stored[g], DMA * b)
                dve.tensor_scalar(lt[:, g, sc, :], ps_l[sc % 2][:, :], 1.0, None, ALU.mult, ALU.max,
                                  accum_out=gmax[:, sc, g:g + 1]).then_inc(logit_out, 1)

            def token_parts(j, par, t):
                if t == 0:
                    dve.wait_ge(xback_loaded[par], DMA * (j // 2 + 1))
                dve.wait_ge(dispatched, GT * j + max(t - 1, 0))
                dve.tensor_copy(xs_hi[t % 2][:, :], xback[par][:, t, :]).then_inc(xs_hi_done, 1)
                dve.wait_ge(xs_hi_done, GT * j + t + 1)
                dve.tensor_tensor(xs_lo[t % 2][:, :], xback[par][:, t, :], rd(xs_hi[t % 2][:, :]),
                                  ALU.subtract).then_inc(xs_done, 1)

            def exp_lo(j, t, h):
                n = HB * (GT * j + t) + h
                dve.wait_ge(e_hi_done, n + 1)
                dve.tensor_tensor(e_lo[t % 2][:, h * BANK:(h + 1) * BANK], ps_t[h][:, :],
                                  rd(e_hi[t % 2][:, h * BANK:(h + 1) * BANK]), ALU.subtract).then_inc(e_lo_done, 1)

            token_stats(0, 0)
            normalize(0, 0)
            token_stats(1, 1)
            normalize(1, 1)
            for k in range(KD):
                transposed_lo(0, 0, k)

            def emit(b, fill, drain):
                for g in range(NG):
                    i = b * NG + g
                    j = i - NG
                    out = (lambda sc: logits_out(b, g, i, sc, drain)) if fill else (lambda sc: None)
                    nxt = fill and exists(b, g, 1)
                    nxt2 = fill and exists(b, g, 2)
                    out(0)
                    if nxt2:
                        token_stats(i + 2, g % 2)
                    out(1)
                    out(2)
                    if nxt:
                        transposed_lo(i + 1, (g + 1) % 2, 0)
                    out(3)
                    if nxt:
                        transposed_lo(i + 1, (g + 1) % 2, 1)
                    out(4)
                    if nxt2:
                        normalize(i + 2, g % 2)
                    out(5)
                    if drain:
                        exp_lo(j, 0, 0)
                    out(6)
                    if drain:
                        exp_lo(j, 0, 1)
                    out(7)
                    if fill and g == NG - 1:
                        dve.wait_ge(logit_out, NSC * (i + 1))
                        if drain:
                            dve.wait_ge(exp_done, NSC * (j + 1))
                        dve.tensor_reduce(neg_max[:, :], gmax[:, :, :], AX_X, ALU.max, negate=True).then_inc(max_done, 1)
                    if drain:
                        token_parts(j, g % 2, 0)
                        for t in range(1, GT):
                            exp_lo(j, t, 0)
                            exp_lo(j, t, 1)
                            token_parts(j, g % 2, t)
                            if g == NG - 1 and t == 1:
                                dve.wait_ge(exp_done, NSC * (j + 1))
                                dve.tensor_reduce(tsum[:, :], gsum[:, :, :], AX_X, ALU.add).then_inc(tsum_done, 1)
                                dve.wait_ge(tsum_done, b)
                                dve.reciprocal(inv[:, :], tsum[:, :]).then_inc(inv_done, 1)
                                dve.wait_ge(inv_done, b)
                                dve.wait_ge(inv_mm, HB * (b - 1))
                                dve.tensor_tensor(diag[:, :, :], c["ident"][:, :].unsqueeze(1).to_broadcast([P, NSC, P]),
                                                  inv[:, :].unsqueeze(2).to_broadcast([P, NSC, P]),
                                                  ALU.mult).then_inc(diag_done, 1)
                        if g == NG - 1:
                            dve.wait_ge(dispatched, GT * (j + 1))
                            dve.wait_ge(inv_out, HB * b)
                            for k in range(KD):
                                for h in range(HB):
                                    dve.tensor_tensor(
                                        slots[:, k, h * (E // HB):(h + 1) * (E // HB), b - 1, :],
                                        ps_s[k * HB + h][:, :].rearrange("p (e s) -> p e s", s=S),
                                        inv_rows[:, h * BANK:(h + 1) * BANK].rearrange("p (e s) -> p e s", s=S),
                                        ALU.mult).then_inc(slots_done, 1)

            batches(dve, emit)

        @block.scalar
        def _(act):
            def transposed_hi(i, par, k):
                act.wait_ge(xT_tr, KD * i + k + 1)
                act.activation(xT_hi[par][:, k, :], ps_t[k][:, :], ACT.Copy).then_inc(xT_hi_done, 1)

            for k in range(KD):
                transposed_hi(0, 0, k)

            def emit(b, fill, drain):
                for g in range(NG):
                    i = b * NG + g
                    j = i - NG
                    if drain:
                        if g == 0:
                            act.wait_ge(max_done, b)
                            act.wait_ge(tsum_done, b - 1)
                        act.wait_ge(e_tr, HB * GT * j)
                        for sc in range(NSC):
                            act.activation(et[:, sc, :], lt[:, g, sc, :], ACT.Exp, bias=neg_max[:, sc:sc + 1],
                                           accum_out=gsum[:, sc, g:g + 1]).then_inc(exp_done, 1)
                    if fill and exists(b, g, 1):
                        for k in range(KD):
                            transposed_hi(i + 1, (g + 1) % 2, k)
                    if drain:
                        for t in range(GT):
                            for h in range(HB):
                                act.wait_ge(e_tr, HB * (GT * j + t) + h + 1)
                                act.activation(e_hi[t % 2][:, h * BANK:(h + 1) * BANK], ps_t[h][:, :],
                                               ACT.Copy).then_inc(e_hi_done, 1)
                        if g == NG - 1:
                            act.wait_ge(slots_done, KD * HB * (b - 1))
                            for h in range(HB):
                                act.wait_ge(inv_mm, HB * (b - 1) + h + 1)
                                act.activation(inv_rows[:, h * BANK:(h + 1) * BANK], ps_t[h][:, :],
                                               ACT.Copy).then_inc(inv_out, 1)

            batches(act, emit)

        @block.tensor
        def _(pe):
            def transpose_tokens(i, par):
                pe.wait_ge(xhat_done, i + 1)
                for k in range(KD):
                    for t in range(GT):
                        mm = pe.transpose(ps_t[k][:, t * P:(t + 1) * P], xhat[par][:, t, k * P:(k + 1) * P],
                                          c["ident"][:, :])
                    mm.then_inc(xT_tr, 1)

            def logits(i, par, sc, start_of_phase):
                if sc == 0:
                    pe.wait_ge(xT_lo_done, KD * (i + 1))
                if not (start_of_phase and sc < 2):
                    pe.wait_ge(logit_out, NSC * i + sc - 1)
                cols = slice(sc * P, (sc + 1) * P)
                for k in range(KD):
                    pe.matmul(ps_l[sc % 2][:, :], c["emb_hi"][:, k, cols], xT_hi[par][:, k, :], start=k == 0, stop=False)
                    pe.matmul(ps_l[sc % 2][:, :], c["emb_hi"][:, k, cols], xT_lo[par][:, k, :], start=False, stop=False)
                    mm = pe.matmul(ps_l[sc % 2][:, :], c["emb_lo"][:, k, cols], xT_hi[par][:, k, :],
                                   start=False, stop=k == KD - 1)
                mm.then_inc(logit_mm, 1)

            def transpose_exp(j, t):
                for h in range(HB):
                    for n in range(BANK // P):
                        mm = pe.transpose(ps_t[h][:, n * P:(n + 1) * P],
                                          et[:, h * (BANK // P) + n, t * P:(t + 1) * P], c["ident"][:, :])
                    mm.then_inc(e_tr, 1)

            def dispatch(b, g, j, t):
                start = g == 0 and t == 0
                if start:
                    pe.wait_ge(slots_done, KD * HB * (b - 1))
                pe.wait_ge(xs_done, GT * j + t + 1)
                pe.wait_ge(e_lo_done, HB * (GT * j + t + 1))
                stop = g == NG - 1 and t == GT - 1
                for k in range(KD):
                    cols = slice(k * P, (k + 1) * P)
                    for h in range(HB):
                        half = slice(h * BANK, (h + 1) * BANK)
                        pe.matmul(ps_s[k * HB + h][:, :], xs_hi[t % 2][:, cols], e_hi[t % 2][:, half], start=start, stop=False)
                        pe.matmul(ps_s[k * HB + h][:, :], xs_hi[t % 2][:, cols], e_lo[t % 2][:, half], start=False, stop=False)
                    for h in range(HB):
                        half = slice(h * BANK, (h + 1) * BANK)
                        mm = pe.matmul(ps_s[k * HB + h][:, :], xs_lo[t % 2][:, cols], e_hi[t % 2][:, half],
                                       start=False, stop=stop)
                mm.then_inc(dispatched, 1)

            transpose_tokens(0, 0)

            def emit(b, fill, drain):
                for g in range(NG):
                    i = b * NG + g
                    j = i - NG
                    begin = isinstance(b, int) and b == 0 and g == 0
                    mm = (lambda sc: logits(i, g % 2, sc, begin)) if fill else (lambda sc: None)
                    nxt = fill and exists(b, g, 1)
                    for sc in range(3):
                        mm(sc)
                    if nxt:
                        pe.wait_ge(xT_lo_done, KD * (i + 1))
                        if drain:
                            pe.wait_ge(e_lo_done, HB * GT * j)
                            if g == 0:
                                pe.wait_ge(inv_out, HB * (b - 1))
                        transpose_tokens(i + 1, (g + 1) % 2)
                    for sc in range(3, 6):
                        mm(sc)
                    if drain:
                        pe.wait_ge(exp_done, NSC * (j + 1))
                        if nxt:
                            pe.wait_ge(xT_lo_done, KD * (i + 2))
                        else:
                            pe.wait_ge(e_lo_done, HB * GT * j)
                            if g == 0:
                                pe.wait_ge(inv_out, HB * (b - 1))
                        transpose_exp(j, 0)
                    for sc in range(6, NSC):
                        mm(sc)
                    if drain:
                        for t in range(GT):
                            pe.wait_ge(e_lo_done, HB * (GT * j + t + 1))
                            if t < GT - 1:
                                transpose_exp(j, t + 1)
                            elif g == NG - 1:
                                pe.wait_ge(diag_done, b)
                                for h in range(HB):
                                    pe.matmul(ps_t[h][:, :], c["ones"][:, :],
                                              diag[:, h * (BANK // P):(h + 1) * (BANK // P), :],
                                              start=True, stop=True).then_inc(inv_mm, 1)
                            dispatch(b, g, j, t)

            batches(pe, emit)


def expert_stage(nc, c, tag, prm, slots, eout):
    with ExitStack() as ctx:
        al = Scope(nc, ctx, tag)
        raw = {n: [al.sb(f"raw_{n}{q}", [P, *shape]) for q in range(2)]
               for n, shape in (("g", (KD, F)), ("u", (KD, F)), ("d", (KF, D)))}
        hi = {n: [al.sb(f"hi_{n}{q}", [P, *shape], F32R) for q in range(2)]
              for n, shape in (("g", (KD, F)), ("u", (KD, F)), ("d", (KF, D)))}
        lo = {n: [al.sb(f"lo_{n}{q}", [P, *shape], F32R) for q in range(2)]
              for n, shape in (("g", (KD, F)), ("u", (KD, F)), ("d", (KF, D)))}
        bd = [al.sb(f"bd{q}", [P, D]) for q in range(2)]
        R = B * S
        in_hi = [al.sb(f"in_hi{q}", [P, KD, R], F32R) for q in range(2)]
        in_lo = [al.sb(f"in_lo{q}", [P, KD, R], F32R) for q in range(2)]
        gel = [al.sb(f"gel{q}", [P, KF, R]) for q in range(2)]
        h_hi = [al.sb(f"h_hi{q}", [P, KF, R], F32R) for q in range(2)]
        h_lo = [al.sb(f"h_lo{q}", [P, KF, R], F32R) for q in range(2)]
        ps_h = [al.ps(f"ps_h{f}", [P, BANK]) for f in range(KF)]
        ps_o = [al.ps(f"ps_o{q}", [P, BANK]) for q in range(2)]
        w_loaded = [al.sem(f"w_loaded{q}") for q in range(2)]
        bd_loaded = [al.sem(f"bd_loaded{q}") for q in range(2)]
        names = ("gate_up_hi", "gate_lo", "up_lo", "down_hi", "down_lo", "in_hi_done", "in_lo_done", "hidden_mm",
                 "gelu_done", "hidden_out", "h_hi_done", "h_lo_done", "down_mm", "eout_done")
        (gate_up_hi, gate_lo, up_lo, down_hi, down_lo, in_hi_done, in_lo_done, hidden_mm,
         gelu_done, hidden_out, h_hi_done, h_lo_done, down_mm, eout_done) = (al.sem(n) for n in names)
        block = ctx.enter_context(nc.Block())
        w_src = {"g": prm["Wg"].rearrange("e (k p) f -> e p k f", p=P), "u": prm["Wu"].rearrange("e (k p) f -> e p k f", p=P),
                 "d": prm["Wd"].rearrange("e (k p) o -> e p k o", p=P)}

        def pairs(eng, emit):
            emit(0, True)
            with eng.Fori(1, E // 2) as pair:
                emit(pair, False)

        @block.sync
        def _(sp):
            def emit(pair, first):
                for q in range(2):
                    e = 2 * pair + q
                    if not first:
                        sp.wait_ge(gate_lo, e - 1)
                        sp.wait_ge(up_lo, e - 1)
                        sp.wait_ge(down_lo, e - 1)
                    for n in "gud":
                        sp.dma_start(raw[n][q][:, :, :], w_src[n][e]).then_inc(w_loaded[q], DMA)
                    if not first:
                        sp.wait_ge(eout_done, B * (e - 1))
                    sp.dma_start(bd[q][:, :], prm["bd"][e].rearrange("(a n) -> a n", a=1).to_broadcast([P, D]))\
                      .then_inc(bd_loaded[q], DMA)

            pairs(sp, emit)

        @block.gpsimd
        def _(pool):
            def emit(pair, first):
                for q in range(2):
                    e = 2 * pair + q
                    if not first:
                        pool.wait_ge(down_mm, e - 1)
                    pool_wait(pool, c, w_loaded[q], 3 * DMA * (pair + 1))
                    pool.tensor_scalar(hi["d"][q][:, :, :], raw["d"][q][:, :, :], 1.0, 0.0, ALU.mult, ALU.add).then_inc(down_hi, 1)
                    pool.wait_ge(gate_up_hi, 2 * (e + 1))
                    pool.tensor_tensor(lo["u"][q][:, :, :], raw["u"][q][:, :, :], rd(hi["u"][q][:, :, :]),
                                       ALU.subtract).then_inc(up_lo, 1)
                    pool.wait_ge(down_hi, e + 1)
                    pool.tensor_tensor(lo["d"][q][:, :, :], raw["d"][q][:, :, :], rd(hi["d"][q][:, :, :]),
                                       ALU.subtract).then_inc(down_lo, 1)

            pairs(pool, emit)

        @block.scalar
        def _(act):
            def weights_hi(e, pair, q, first):
                act.wait_ge(w_loaded[q], 3 * DMA * (pair + 1))
                if not first:
                    act.wait_ge(hidden_mm, KF * (e - 1))
                for n in "gu":
                    act.activation(hi[n][q][:, :, :], raw[n][q][:, :, :], ACT.Copy).then_inc(gate_up_hi, 1)
                act.activation(in_hi[q][:, :, :].rearrange("p k (b s) -> p k b s", s=S), slots[:, :, e, :, :],
                               ACT.Copy).then_inc(in_hi_done, 1)

            weights_hi(0, 0, 0, True)

            def emit(pair, first, last):
                for q in range(2):
                    e = 2 * pair + q
                    if not (last and q == 1):
                        weights_hi(e + 1, pair + q, 1 - q, first and q == 0)
                    for f in range(KF):
                        act.wait_ge(hidden_mm, KF * e + f + 1)
                        if f == 0 and not first:
                            act.wait_ge(h_lo_done, e - 1)
                        act.activation(gel[q][:, f, :], ps_h[f][:, 0:R], ACT.Gelu,
                                       bias=c["biases"][:, bass.ds(e * KF + f, 1)]).then_inc(gelu_done, 1)
                    act.wait_ge(hidden_out, KF * (e + 1))
                    if not first:
                        act.wait_ge(down_mm, e - 1)
                    act.activation(h_hi[q][:, :, :], gel[q][:, :, :], ACT.Copy).then_inc(h_hi_done, 1)

            emit(0, True, False)
            with act.Fori(1, E // 2 - 1) as pair:
                emit(pair, False, False)
            emit(E // 2 - 1, False, True)

        @block.vector
        def _(dve):
            def parts_lo(e, q):
                dve.wait_ge(gate_up_hi, 2 * e + 1)
                dve.tensor_tensor(lo["g"][q][:, :, :], raw["g"][q][:, :, :], rd(hi["g"][q][:, :, :]),
                                  ALU.subtract).then_inc(gate_lo, 1)
                dve.wait_ge(in_hi_done, e + 1)
                for k in range(KD):
                    last = dve.tensor_tensor(in_lo[q][:, k, :].rearrange("p (b s) -> p b s", s=S), slots[:, k, e, :, :],
                                             rd(in_hi[q][:, k, :]).rearrange("p (b s) -> p b s", s=S), ALU.subtract)
                last.then_inc(in_lo_done, 1)

            def rows_out(e, pair, q):
                dve.wait_ge(down_mm, e + 1)
                dve.wait_ge(bd_loaded[q], DMA * (pair + 1))
                for b in range(B):
                    half = slice((b % 2) * S, (b % 2) * S + S)
                    dve.tensor_tensor(eout[q * S:(q + 1) * S, b, pair, :], ps_o[q][half, (b // 2) * D:(b // 2 + 1) * D],
                                      bd[q][half, :], ALU.add).then_inc(eout_done, 1)

            parts_lo(0, 0)

            def emit(pair, first, last):
                for q in range(2):
                    e = 2 * pair + q
                    if not (last and q == 1):
                        parts_lo(e + 1, 1 - q)
                    for f in range(KF):
                        dve.wait_ge(gelu_done, KF * e + f + 1)
                        dve.scalar_tensor_tensor(out=gel[q][:, f, :], in0=ps_h[f][:, R:2 * R],
                                                 scalar=c["biases"][:, bass.ds(E * KF + e * KF + f, 1)],
                                                 in1=gel[q][:, f, :], op0=ALU.add, op1=ALU.mult).then_inc(hidden_out, 1)
                    dve.wait_ge(h_hi_done, e + 1)
                    dve.tensor_tensor(h_lo[q][:, :, :], gel[q][:, :, :], rd(h_hi[q][:, :, :]), ALU.subtract).then_inc(h_lo_done, 1)
                    if not (first and q == 0):
                        rows_out(e - 1, pair - 1 + q, 1 - q)

            emit(0, True, False)
            with dve.Fori(1, E // 2 - 1) as pair:
                emit(pair, False, False)
            emit(E // 2 - 1, False, True)
            rows_out(E - 1, E // 2 - 1, 1)

        @block.tensor
        def _(pe):
            def hidden(e, q, first):
                pe.wait_ge(gate_lo, e + 1)
                pe.wait_ge(up_lo, e + 1)
                pe.wait_ge(in_lo_done, e + 1)
                for f in range(KF):
                    if not (first and q == 0):
                        pe.wait_ge(hidden_out, KF * (e - 1) + f + 1)
                    cols = slice(f * P, (f + 1) * P)
                    for i, n in enumerate("gu"):
                        out = ps_h[f][:, i * R:(i + 1) * R]
                        for k in range(KD):
                            pe.matmul(out, hi[n][q][:, k, cols], in_hi[q][:, k, :], start=k == 0, stop=False)
                            pe.matmul(out, hi[n][q][:, k, cols], in_lo[q][:, k, :], start=False, stop=False)
                            mm = pe.matmul(out, lo[n][q][:, k, cols], in_hi[q][:, k, :], start=False, stop=k == KD - 1)
                    mm.then_inc(hidden_mm, 1)

            def down(e, q, first):
                pe.wait_ge(h_lo_done, e + 1)
                pe.wait_ge(down_lo, e + 1)
                if not first:
                    pe.wait_ge(eout_done, B * (e - 1))
                for r in range(R // P):
                    out, rows = ps_o[q][:, r * D:(r + 1) * D], slice(r * P, (r + 1) * P)
                    for f in range(KF):
                        pe.matmul(out, h_hi[q][:, f, rows], hi["d"][q][:, f, :], start=f == 0, stop=False)
                        pe.matmul(out, h_hi[q][:, f, rows], lo["d"][q][:, f, :], start=False, stop=False)
                        mm = pe.matmul(out, h_lo[q][:, f, rows], hi["d"][q][:, f, :], start=False, stop=f == KF - 1)
                mm.then_inc(down_mm, 1)

            hidden(0, 0, True)
            hidden(1, 1, True)
            down(0, 0, True)
            with pe.Fori(1, E // 2) as pair:
                hidden(2 * pair, 0, False)
                down(2 * pair - 1, 1, False)
                hidden(2 * pair + 1, 1, False)
                down(2 * pair, 0, False)
            down(E - 1, 1, False)


def combine_stage(nc, c, tag, x_in, x_out, logits_dram, eout):
    NT = T // P
    with ExitStack() as ctx:
        al = Scope(nc, ctx, tag)
        lt = [al.sb(f"lt{i}", [P, NSC, GN]) for i in range(2)]
        xin = [al.sb(f"xin{i}", [P, GT, D]) for i in range(2)]
        xout = [al.sb(f"xout{i}", [P, GT, D]) for i in range(2)]
        ex = [al.sb(f"ex{i}", [P, SL]) for i in range(2)]
        eT_hi = [al.sb(f"eT_hi{i}", [P, NSC, P], F32R) for i in range(2)]
        eT_lo = [al.sb(f"eT_lo{i}", [P, NSC, P], F32R) for i in range(2)]
        eo = al.sb("eo", [P, 2, NSC, 2, D], F32R)
        neg_max, sums = [al.sb(f"neg_max{i}", [P, 1]) for i in range(2)], [al.sb(f"sums{i}", [P, 1]) for i in range(4)]
        twice, half_inv = [al.sb(f"twice{i}", [P, 1]) for i in range(4)], [al.sb(f"half_inv{i}", [P, 1]) for i in range(4)]
        cross, weighted = [al.sb(f"cross{i}", [P, D]) for i in range(2)], [al.sb(f"weighted{i}", [P, D]) for i in range(2)]
        ps_l = al.ps("ps_l", [P, HB * BANK])
        ps_e = [al.ps(f"ps_e{i}", [P, HB * BANK]) for i in range(2)]
        ps_y = [al.ps(f"ps_y{i}", [P, BANK]) for i in range(2)]
        lt_loaded = [al.sem(f"lt_loaded{i}") for i in range(2)]
        x_loaded = [al.sem(f"x_loaded{i}") for i in range(2)]
        stored = [al.sem(f"stored{i}") for i in range(2)]
        names = ("l_tr", "max_done", "exp_done", "e_tr", "e_hi_done", "e_lo_done", "twice_done", "inv_done", "mixed",
                 "cross_done", "weighted_done", "sum_done", "eo_hi_done", "eo_lo_done")
        (l_tr, max_done, exp_done, e_tr, e_hi_done, e_lo_done, twice_done, inv_done, mixed,
         cross_done, weighted_done, sum_done, eo_hi_done, eo_lo_done) = (al.sem(n) for n in names)
        block = ctx.enter_context(nc.Block())
        LAST = B * NT - 1

        def batches(eng, emit):
            emit(0, False)
            with eng.Fori(1, B - 1) as b:
                emit(b, False)
            emit(B - 1, True)

        @block.sync
        def _(sp):
            x_g = x_in.rearrange("b (g p t) d -> (b g) p t d", g=NG, t=GT)
            y_g = x_out.rearrange("b (g p t) d -> (b g) p t d", g=NG, t=GT)

            def load(i, par):
                sp.dma_start(lt[par][:, :, :], logits_dram[i]).then_inc(lt_loaded[par], DMA)
                sp.dma_start(xin[par][:, :, :], x_g[i]).then_inc(x_loaded[par], DMA)

            load(0, 0)
            load(1, 1)

            def emit(b, last):
                for g in range(NG):
                    i = b * NG + g
                    sp.wait_ge(sum_done, GT * (i + 1))
                    sp.dma_start(y_g[i], xout[g % 2][:, :, :]).then_inc(stored[g % 2], DMA)
                    if not (last and g >= NG - 2):
                        sp.wait_ge(l_tr, HB * GT * (i + 1))
                        load(i + 2, g % 2)

            batches(sp, emit)
            for s in stored:
                sp.wait_ge(s, B * NG // 2 * DMA)

        @block.gpsimd
        def _(pool):
            def emit(b, last):
                for g in range(NG):
                    i = b * NG + g
                    pool.wait_ge(x_loaded[g % 2], DMA * (2 * b + g // 2 + 1))
                    if g >= 2 or not (isinstance(b, int) and b == 0):
                        pool.wait_ge(stored[g % 2], DMA * (2 * b + g // 2))
                    for t in range(GT):
                        pool.wait_ge(weighted_done, GT * i + t + 1)
                        pool.tensor_tensor(xout[g % 2][:, t, :], xin[g % 2][:, t, :], weighted[t % 2][:, :],
                                           ALU.add).then_inc(sum_done, 1)

            batches(pool, emit)

        @block.vector
        def _(dve):
            def slot_out_lo(b, par, rows):
                for n in rows:
                    dve.wait_ge(eo_hi_done, NSC * b + n + 1)
                    dve.tensor_tensor(eo[:, par, n, 1, :], eout[:, b, n, :], rd(eo[:, par, n, 0, :]),
                                      ALU.subtract).then_inc(eo_lo_done, 1)

            def row_max(n, m):
                dve.wait_ge(l_tr, HB * (n + 1))
                if m >= 2:
                    dve.wait_ge(exp_done, n - 1)
                dve.tensor_reduce(neg_max[m % 2][:, :], ps_l[:, :], AX_X, ALU.max, negate=True).then_inc(max_done, 1)

            def parts_lo(n, m):
                for h in range(HB):
                    dve.wait_ge(e_hi_done, HB * n + h + 1)
                    dve.tensor_tensor(eT_lo[m % 2][:, h * (NSC // HB):(h + 1) * (NSC // HB), :],
                                      ps_e[m % 2][:, h * BANK:(h + 1) * BANK].rearrange("p (c t) -> p c t", t=P),
                                      rd(eT_hi[m % 2][:, h * (NSC // HB):(h + 1) * (NSC // HB), :]),
                                      ALU.subtract).then_inc(e_lo_done, 1)

            def half_inverse(n, m):
                dve.wait_ge(exp_done, n + 1)
                dve.tensor_scalar(twice[m % 4][:, :], sums[m % 4][:, :], 2.0, None, ALU.mult).then_inc(twice_done, 1)
                dve.wait_ge(twice_done, n + 1)
                dve.reciprocal(half_inv[m % 4][:, :], twice[m % 4][:, :]).then_inc(inv_done, 1)

            def weigh(n, m):
                dve.wait_ge(cross_done, n + 1)
                if m >= 2:
                    dve.wait_ge(sum_done, n - 1)
                dve.scalar_tensor_tensor(out=weighted[m % 2][:, :], in0=ps_y[m % 2][:, 0:D], scalar=half_inv[m % 4][:, :],
                                         in1=cross[m % 2][:, :], op0=ALU.mult, op1=ALU.add).then_inc(weighted_done, 1)

            slot_out_lo(0, 0, range(NSC))
            row_max(0, 0)
            row_max(1, 1)
            parts_lo(0, 0)
            half_inverse(0, 0)

            def emit(b, last):
                for t in range(NT):
                    n = b * NT + t
                    m = n if isinstance(n, int) else t + NT
                    if not (last and t >= NT - 2):
                        row_max(n + 2, m + 2)
                    if not (last and t >= NT - 1):
                        parts_lo(n + 1, m + 1)
                        half_inverse(n + 1, m + 1)
                    if not last and t % 2 == 0:
                        slot_out_lo(b + 1, (b + 1) % 2, range(t // 2, t // 2 + 1))
                    weigh(n, m)

            batches(dve, emit)

        @block.scalar
        def _(act):
            def slot_out_hi(b, par, rows, first):
                for n in rows:
                    if not first and n == 0:
                        act.wait_ge(mixed, NT * (b - 1))
                    act.activation(eo[:, par, n, 0, :], eout[:, b, n, :], ACT.Copy).then_inc(eo_hi_done, 1)

            def exponentials(n, m):
                act.wait_ge(max_done, n + 1)
                if m >= 2:
                    act.wait_ge(e_tr, HB * (n - 1))
                if m >= 4:
                    act.wait_ge(inv_done, n - 3)
                act.activation(ex[m % 2][:, :], ps_l[:, :], ACT.Exp, bias=neg_max[m % 2][:, :],
                               accum_out=sums[m % 4][:, :]).then_inc(exp_done, 1)

            def parts_hi(n, m):
                for h in range(HB):
                    act.wait_ge(e_tr, HB * n + h + 1)
                    if m >= 2 and h == 0:
                        act.wait_ge(mixed, n - 1)
                    act.activation(eT_hi[m % 2][:, h * (NSC // HB):(h + 1) * (NSC // HB), :],
                                   ps_e[m % 2][:, h * BANK:(h + 1) * BANK].rearrange("p (c t) -> p c t", t=P),
                                   ACT.Copy).then_inc(e_hi_done, 1)

            def cross_terms(n, m):
                act.wait_ge(mixed, n + 1)
                act.wait_ge(inv_done, n + 1)
                if m >= 2:
                    act.wait_ge(weighted_done, n - 1)
                act.activation(cross[m % 2][:, :], ps_y[m % 2][:, D:2 * D], ACT.Copy,
                               scale=half_inv[m % 4][:, :]).then_inc(cross_done, 1)

            slot_out_hi(0, 0, range(NSC), True)
            exponentials(0, 0)
            exponentials(1, 1)
            parts_hi(0, 0)

            def emit(b, last):
                for t in range(NT):
                    n = b * NT + t
                    m = n if isinstance(n, int) else t + NT
                    if not (last and t >= NT - 1):
                        parts_hi(n + 1, m + 1)
                    if not (last and t >= NT - 2):
                        exponentials(n + 2, m + 2)
                    if not last and t % 2 == 0:
                        slot_out_hi(b + 1, (b + 1) % 2, range(t // 2, t // 2 + 1), isinstance(b, int) and b == 0)
                    cross_terms(n, m)

            batches(act, emit)

        @block.tensor
        def _(pe):
            def transpose_logits(n, m):
                g_par, t = (m // GT) % 2, m % GT
                if t == 0:
                    gi = n // GT
                    pe.wait_ge(lt_loaded[g_par], DMA * (gi // 2 + 1) if isinstance(n, int) else group_loads(n))
                if m >= 1:
                    pe.wait_ge(exp_done, n)
                for h in range(HB):
                    for j in range(NSC // HB):
                        sc = h * (NSC // HB) + j
                        mm = pe.transpose(ps_l[:, sc * P:(sc + 1) * P], lt[g_par][:, sc, t * P:(t + 1) * P],
                                          c["ident"][:, :])
                    mm.then_inc(l_tr, 1)

            def group_loads(n):
                return (n // (2 * GT) + 1) * DMA

            def transpose_exp(n, m):
                pe.wait_ge(exp_done, n + 1)
                if m >= 2:
                    pe.wait_ge(e_lo_done, HB * (n - 1))
                for h in range(HB):
                    for j in range(NSC // HB):
                        sc = h * (NSC // HB) + j
                        mm = pe.transpose(ps_e[m % 2][:, sc * P:(sc + 1) * P], ex[m % 2][:, sc * P:(sc + 1) * P],
                                          c["ident"][:, :])
                    mm.then_inc(e_tr, 1)

            def mix(n, m, par):
                pe.wait_ge(e_lo_done, HB * (n + 1))
                if m >= 2:
                    pe.wait_ge(weighted_done, n - 1)
                for sc in range(NSC):
                    pe.matmul(ps_y[m % 2][:, :], eT_hi[m % 2][:, sc, :],
                              eo[:, par, sc, :, :].rearrange("p a d -> p (a d)"),
                              start=sc == 0, stop=sc == NSC - 1, skip_group_check=True)
                    mm = pe.matmul(ps_y[m % 2][:, 0:D], eT_lo[m % 2][:, sc, :], eo[:, par, sc, 0, :],
                                   start=False, stop=sc == NSC - 1, skip_group_check=True)
                mm.then_inc(mixed, 1)

            transpose_logits(0, 0)
            transpose_logits(1, 1)
            transpose_exp(0, 0)

            def emit(b, last):
                for t in range(NT):
                    n = b * NT + t
                    m = n if isinstance(n, int) else t + NT
                    if not (last and t >= NT - 2):
                        transpose_logits(n + 2, m + 2)
                    if not (last and t >= NT - 1):
                        transpose_exp(n + 1, m + 1)
                    if t == 0:
                        pe.wait_ge(eo_lo_done, NSC * (b + 1))
                    mix(n, m, b % 2)

            batches(pe, emit)


def attention_stage(nc, c, tag, prm, x_in, x_out):
    NGR = B * NG
    with ExitStack() as ctx:
        al = Scope(nc, ctx, tag)
        w_raw = {n: al.sb(f"w_{n}", [P, KD, D]) for n in "qkvgo"}
        w_hi = {n: al.sb(f"hi_{n}", [P, KD, D], F32R) for n in "mvgo"}
        w_lo = {n: al.sb(f"lo_{n}", [P, KD, D], F32R) for n in "mvgo"}
        ld, zcol = al.sb("ld", [P, 1]), al.sb("zcol", [P, 6])
        steps, mask = al.sb("steps", [P, P]), al.sb("mask", [P, P])
        xin = [al.sb(f"xin{i}", [P, GT, D]) for i in range(2)]
        xn = [al.sb(f"xn{i}", [P, GT, D]) for i in range(2)]
        base = [al.sb(f"base{i}", [P, GT, D]) for i in range(2)]
        xout = [al.sb(f"xout{i}", [P, GT, D]) for i in range(2)]
        xT_hi = [al.sb(f"xT_hi{i}", [P, KD, GN], F32R) for i in range(2)]
        xT_lo = [al.sb(f"xT_lo{i}", [P, KD, GN], F32R) for i in range(2)]
        qT_hi, qT_lo = al.sb("qT_hi", [P, KD, GN], F32R), al.sb("qT_lo", [P, KD, GN], F32R)
        v_hi, v_lo = al.sb("v_hi", [P, GT, D], F32R), al.sb("v_lo", [P, GT, D], F32R)
        gate = [al.sb(f"gate{i}", [P, KD, GN]) for i in range(2)]
        sc, s_hi, s_lo = al.sb("sc", [P, GT, P]), al.sb("s_hi", [P, GT, P], F32R), al.sb("s_lo", [P, GT, P], F32R)
        o, o_hi, o_lo = al.sb("o", [P, KD, GN]), al.sb("o_hi", [P, KD, GN], F32R), al.sb("o_lo", [P, KD, GN], F32R)
        stats, mv = al.sb("stats", [P, GT, 6]), [al.sb(f"mv{i}", [P, GT, 2]) for i in range(2)]
        var_eps, rstd = al.sb("var_eps", [P, GT]), [al.sb(f"rstd{i}", [P, GT]) for i in range(2)]
        ps = [al.ps(f"ps{i}", [P, BANK]) for i in range(8)]
        ps_t, ps_q, ps_v, ps_g = ps[0:2], ps[2:4], ps[4:6], ps[6:8]

        def weights_block():
            with ExitStack() as wctx:
                wa = Scope(nc, wctx, tag + "w_")
                loaded, w_tr, hi_done, lo_done = (wa.sem(n) for n in ("loaded", "w_tr", "hi_done", "lo_done"))
                z_step, a_step, steps_done, mask_done = (wa.sem(n) for n in ("z_step", "a_step", "steps_done", "mask_done"))
                block = wctx.enter_context(nc.Block())
                jobs = [(n, k) for n in "mvgo" for k in range(KD)]

                @block.sync
                def _(sp):
                    for n in "qkvgo":
                        sp.dma_start(w_raw[n][:, :, :], prm["W_" + n].rearrange("(k p) d -> p k d", p=P)).then_inc(loaded, DMA)
                    sp.dma_start(ld[:, :], prm["log_decay"][0:1].rearrange("(a n) -> a n", a=1).to_broadcast([P, 1]))                      .then_inc(loaded, DMA)
                    sp.wait_ge(loaded, 6 * DMA)

                @block.gpsimd
                def _(pool):
                    pool.iota(steps[:, :], [[1, P]], base=0, channel_multiplier=-1,
                              allow_small_or_imprecise_dtypes=True).then_inc(steps_done, 1)
                    pool.wait_ge(a_step, 3)
                    blocks = mask[:, :].rearrange("p (c i) -> p c i", i=CHUNK)
                    pool.affine_select(out=mask[:, :], in_=mask[:, :], compare_op=ALU.is_ge, fill=0.0, base=0,
                                       pattern=[[1, P]], channel_multiplier=-1).then_inc(mask_done, 1)
                    pool.wait_ge(mask_done, 1)
                    pool.affine_select(out=blocks, in_=blocks, compare_op=ALU.is_ge, fill=0.0, base=0,
                                       pattern=[[-CHUNK, P // CHUNK], [0, CHUNK]], channel_multiplier=1).then_inc(mask_done, 1)

                @block.scalar
                def _(act):
                    act.wait_ge(z_step, 2)
                    act.activation(zcol[:, 2:3], zcol[:, 1:2], ACT.Exp, scale=-1.0).then_inc(a_step, 1)
                    act.wait_ge(a_step, 1)
                    act.activation(zcol[:, 3:4], zcol[:, 2:3], ACT.Ln, bias=c["ones"][:, 0:1]).then_inc(a_step, 1)
                    act.wait_ge(z_step, 5)
                    act.activation(mask[:, :], steps[:, :], ACT.Exp, scale=zcol[:, 4:5]).then_inc(a_step, 1)
                    for n, (w, k) in enumerate(jobs):
                        act.wait_ge(w_tr, n + 1)
                        act.activation(w_hi[w][:, k, :], ps[n][:, 0:D], ACT.Copy).then_inc(hi_done, 1)

                @block.vector
                def _(dve):
                    dve.wait_ge(loaded, 6 * DMA)
                    dve.tensor_scalar(zcol[:, 0:1], ld[:, :], -1.0, 0.0, ALU.mult, ALU.max).then_inc(z_step, 1)
                    dve.wait_ge(z_step, 1)
                    dve.scalar_tensor_tensor(out=zcol[:, 1:2], in0=zcol[:, 0:1], scalar=2.0, in1=ld[:, :],
                                             op0=ALU.mult, op1=ALU.add).then_inc(z_step, 1)
                    dve.wait_ge(a_step, 2)
                    dve.tensor_tensor(zcol[:, 5:6], zcol[:, 0:1], zcol[:, 3:4], ALU.add).then_inc(z_step, 1)
                    dve.wait_ge(z_step, 3)
                    dve.tensor_scalar(zcol[:, 4:5], zcol[:, 5:6], -1.0, None, ALU.mult).then_inc(z_step, 1)
                    dve.wait_ge(steps_done, 1)
                    dve.tensor_scalar(steps[:, :], steps[:, :], 0.0, None, ALU.max).then_inc(z_step, 1)
                    for n, (w, k) in enumerate(jobs):
                        dve.wait_ge(hi_done, n + 1)
                        dve.tensor_tensor(w_lo[w][:, k, :], ps[n][:, 0:D], rd(w_hi[w][:, k, :]), ALU.subtract).then_inc(lo_done, 1)

                @block.tensor
                def _(pe):
                    pe.wait_ge(loaded, 6 * DMA)
                    for n, (w, k) in enumerate(jobs):
                        cols = slice(k * P, (k + 1) * P)
                        for j in range(KD):
                            if w == "m":
                                mm = pe.matmul(ps[n][:, 0:D], w_raw["q"][:, j, cols], w_raw["k"][:, j, :],
                                               start=j == 0, stop=j == KD - 1)
                            else:
                                mm = pe.transpose(ps[n][:, j * P:(j + 1) * P], w_raw[w][:, j, cols], c["ident"][:, :])
                        mm.then_inc(w_tr, 1)

        weights_block()
        x_loaded = [al.sem(f"x_loaded{i}") for i in range(2)]
        stored = [al.sem(f"stored{i}") for i in range(2)]
        names = ("stats_done", "mv_done", "var_done", "rstd_done", "xn_done", "base_done", "xT_tr", "xT_hi_done",
                 "xT_lo_done", "q_mm", "q_hi_done", "q_lo_done", "gate_mm", "gate_done", "v_mm", "v_hi_done", "v_lo_done",
                 "s_mm", "s_masked", "s_hi_done", "s_lo_done", "o_mm", "o_gated", "o_hi_done", "o_lo_done", "y_mm", "y_done")
        (stats_done, mv_done, var_done, rstd_done, xn_done, base_done, xT_tr, xT_hi_done,
         xT_lo_done, q_mm, q_hi_done, q_lo_done, gate_mm, gate_done, v_mm, v_hi_done, v_lo_done,
         s_mm, s_masked, s_hi_done, s_lo_done, o_mm, o_gated, o_hi_done, o_lo_done, y_mm, y_done) = (al.sem(n) for n in names)
        block = ctx.enter_context(nc.Block())

        def groups(eng, emit):
            emit(0, 0, False, 2)
            emit(1, 1, True, 2)
            with eng.Fori(1, NGR // 2 - 1) as pair:
                for q in range(2):
                    emit(2 * pair + q, q, True, 2)
            emit(NGR - 2, 0, True, 1)
            emit(NGR - 1, 1, True, 0)

        @block.sync
        def _(sp):
            x_g = x_in.rearrange("b (g t p) d -> (b g) p t d", g=NG, t=GT)
            y_g = x_out.rearrange("b (g t p) d -> (b g) p t d", g=NG, t=GT)
            for n in range(2):
                sp.dma_start(xin[n][:, :, :], x_g[n]).then_inc(x_loaded[n], DMA)

            def emit(g, q, before, ahead):
                if ahead == 2:
                    sp.wait_ge(base_done, g + 1)
                    sp.dma_start(xin[q][:, :, :], x_g[g + 2]).then_inc(x_loaded[q], DMA)
                if before:
                    sp.wait_ge(y_done, KD * g)
                    sp.dma_start(y_g[g - 1], xout[1 - q][:, :, :]).then_inc(stored[1 - q], DMA)

            groups(sp, emit)
            sp.wait_ge(y_done, KD * NGR)
            sp.dma_start(y_g[NGR - 1], xout[1][:, :, :]).then_inc(stored[1], DMA)
            for s in stored:
                sp.wait_ge(s, NGR // 2 * DMA)

        @block.gpsimd
        def _(pool):
            def norm_scale(g, q):
                pool_wait(pool, c, mv_done, GT * (g + 1))
                pool.tensor_scalar(var_eps[:, :], mv[q][:, :, 1], 1.0, EPS, ALU.mult, ALU.add).then_inc(var_done, 1)
                pool.wait_ge(var_done, g + 1)
                pool.tensor_tensor(rstd[q][:, :], var_eps[:, :], c["minus_half"][:, 0:GT], ALU.pow).then_inc(rstd_done, 1)

            def residual(g, q, first):
                pool.wait_ge(xn_done, g + 1)
                if not first:
                    pool.wait_ge(y_done, KD * (g - 1))
                pool.tensor_tensor(base[q][:, :, :], xin[q][:, :, :], xn[q][:, :, :], ALU.add).then_inc(base_done, 1)

            norm_scale(0, 0)
            residual(0, 0, True)

            def emit(g, q, before, ahead):
                if ahead >= 1:
                    norm_scale(g + 1, 1 - q)
                    residual(g + 1, 1 - q, not before)

            groups(pool, emit)

        @block.vector
        def _(dve):
            def token_stats(g, q):
                dve.wait_ge(x_loaded[q], DMA * (g // 2 + 1))
                for t in range(GT):
                    dve.bn_stats(stats[:, t, :], xin[q][:, t, :]).then_inc(stats_done, 1)
                dve_wait(dve, c, stats_done, GT * (g + 1))
                for t in range(GT):
                    dve.bn_aggr(mv[q][:, t, :], stats[:, t, :]).then_inc(mv_done, 1)

            def normalize(g, q, first):
                dve.wait_ge(rstd_done, g + 1)
                dve.wait_ge(mv_done, GT * (g + 1))
                if not first:
                    dve.wait_ge(xT_tr, KD * (g - 1))
                    dve.wait_ge(base_done, g - 1)
                for t in range(GT):
                    last = dve.tensor_scalar(xn[q][:, t, :], xin[q][:, t, :], mv[q][:, t, 0:1],
                                             rstd[q][:, t:t + 1], ALU.subtract, ALU.mult)
                last.then_inc(xn_done, 1)

            def minus_hi(lo, src, hi, ready, count, done):
                dve.wait_ge(ready, count)
                dve.tensor_tensor(lo, src, rd(hi), ALU.subtract).then_inc(done, 1)

            def tokens_lo(g, q):
                for k in range(KD):
                    minus_hi(xT_lo[q][:, k, :], ps_t[k][:, :], xT_hi[q][:, k, :], xT_hi_done, KD * g + k + 1, xT_lo_done)

            def scores(g):
                dve.wait_ge(s_mm, g + 1)
                dve.tensor_tensor(sc[:, :, :], ps_g[0][:, :].rearrange("p (t n) -> p t n", n=P),
                                  mask[:, :].unsqueeze(1).to_broadcast([P, GT, P]), ALU.mult).then_inc(s_masked, 1)
                minus_hi(s_lo[:, :, :], sc[:, :, :], s_hi[:, :, :], s_hi_done, g + 1, s_lo_done)

            def gated(g, q):
                dve.wait_ge(gate_done, KD * (g + 1))
                for k in range(KD):
                    dve.wait_ge(o_mm, KD * g + k + 1)
                    dve.tensor_tensor(o[:, k, :], ps_v[k][:, :], gate[q][:, k, :], ALU.mult).then_inc(o_gated, 1)

            def gated_lo(g):
                for k in range(KD):
                    minus_hi(o_lo[:, k, :], o[:, k, :], o_hi[:, k, :], o_hi_done, KD * g + k + 1, o_lo_done)

            def finish(g, q, first):
                dve.wait_ge(base_done, g + 1)
                if not first:
                    dve.wait_ge(stored[q], DMA * (g // 2))
                for h in range(KD):
                    dve.wait_ge(y_mm, KD * g + h + 1)
                    dve.tensor_tensor(xout[q][:, 2 * h:2 * h + 2, :], ps_t[h][:, :].rearrange("p (t d) -> p t d", d=D),
                                      base[q][:, 2 * h:2 * h + 2, :], ALU.add).then_inc(y_done, 1)

            token_stats(0, 0)
            normalize(0, 0, True)
            tokens_lo(0, 0)

            def emit(g, q, before, ahead):
                if ahead >= 1:
                    token_stats(g + 1, 1 - q)
                for k in range(KD):
                    minus_hi(qT_lo[:, k, :], ps_q[k][:, :], qT_hi[:, k, :], q_hi_done, KD * g + k + 1, q_lo_done)
                if ahead >= 1:
                    normalize(g + 1, 1 - q, not before)
                if before:
                    gated(g - 1, 1 - q)
                    gated_lo(g - 1)
                if ahead >= 1:
                    tokens_lo(g + 1, 1 - q)
                for h in range(KD):
                    minus_hi(v_lo[:, 2 * h:2 * h + 2, :], ps_v[h][:, :].rearrange("p (t d) -> p t d", d=D),
                             v_hi[:, 2 * h:2 * h + 2, :], v_hi_done, KD * g + h + 1, v_lo_done)
                if before:
                    finish(g - 1, 1 - q, not isinstance(g, int) and False or (isinstance(g, int) and g <= 2))
                scores(g)

            groups(dve, emit)
            gated(NGR - 1, 1)
            gated_lo(NGR - 1)
            finish(NGR - 1, 1, False)

        @block.scalar
        def _(act):
            def tokens_hi(g, q):
                for k in range(KD):
                    act.wait_ge(xT_tr, KD * g + k + 1)
                    act.activation(xT_hi[q][:, k, :], ps_t[k][:, :], ACT.Copy).then_inc(xT_hi_done, 1)

            def gated_hi(g):
                for k in range(KD):
                    act.wait_ge(o_gated, KD * g + k + 1)
                    act.activation(o_hi[:, k, :], o[:, k, :], ACT.Copy).then_inc(o_hi_done, 1)

            tokens_hi(0, 0)

            def emit(g, q, before, ahead):
                for k in range(KD):
                    act.wait_ge(q_mm, KD * g + k + 1)
                    act.activation(qT_hi[:, k, :], ps_q[k][:, :], ACT.Copy).then_inc(q_hi_done, 1)
                if before:
                    gated_hi(g - 1)
                for k in range(KD):
                    act.wait_ge(gate_mm, KD * g + k + 1)
                    act.activation(gate[q][:, k, :], ps_g[k][:, :], ACT.Sigmoid).then_inc(gate_done, 1)
                if ahead >= 1:
                    tokens_hi(g + 1, 1 - q)
                for h in range(KD):
                    act.wait_ge(v_mm, KD * g + h + 1)
                    act.activation(v_hi[:, 2 * h:2 * h + 2, :], ps_v[h][:, :].rearrange("p (t d) -> p t d", d=D),
                                   ACT.Copy).then_inc(v_hi_done, 1)
                act.wait_ge(s_masked, g + 1)
                act.activation(s_hi[:, :, :], sc[:, :, :], ACT.Copy).then_inc(s_hi_done, 1)

            groups(act, emit)
            gated_hi(NGR - 1)

        @block.tensor
        def _(pe):
            def three(out, a_hi, a_lo, b_hi, b_lo, start, stop):
                pe.matmul(out, a_hi, b_hi, start=start, stop=False)
                pe.matmul(out, a_hi, b_lo, start=False, stop=False)
                return pe.matmul(out, a_lo, b_hi, start=False, stop=stop)

            def transpose_tokens(g, q):
                pe.wait_ge(xn_done, g + 1)
                for k in range(KD):
                    for t in range(GT):
                        mm = pe.transpose(ps_t[k][:, t * P:(t + 1) * P], xn[q][:, t, k * P:(k + 1) * P], c["ident"][:, :])
                    mm.then_inc(xT_tr, 1)

            def project(banks, w, q, done):
                for m in range(KD):
                    cols = slice(m * P, (m + 1) * P)
                    for k in range(KD):
                        mm = three(banks[m][:, :], w_hi[w][:, k, cols], w_lo[w][:, k, cols],
                                   xT_hi[q][:, k, :], xT_lo[q][:, k, :], k == 0, k == KD - 1)
                    mm.then_inc(done, 1)

            def rows(banks, a_hi, a_lo, w, done):
                for t in range(GT):
                    out = banks[t // 2][:, (t % 2) * D:(t % 2 + 1) * D]
                    for k in range(KD):
                        mm = three(out, a_hi[:, k, t * P:(t + 1) * P], a_lo[:, k, t * P:(t + 1) * P],
                                   w_hi[w][:, k, :], w_lo[w][:, k, :], k == 0, k == KD - 1)
                    if t % 2:
                        mm.then_inc(done, 1)

            def mix_values(g):
                pe.wait_ge(s_lo_done, g + 1)
                pe.wait_ge(v_lo_done, KD * (g + 1))
                for k in range(KD):
                    cols = slice(k * P, (k + 1) * P)
                    for t in range(GT):
                        mm = three(ps_v[k][:, t * P:(t + 1) * P], v_hi[:, t, cols], v_lo[:, t, cols],
                                   s_hi[:, t, :], s_lo[:, t, :], True, True)
                    mm.then_inc(o_mm, 1)

            transpose_tokens(0, 0)

            def emit(g, q, before, ahead):
                pe.wait_ge(xT_lo_done, KD * (g + 1))
                pe.wait_ge(q_lo_done, KD * g)
                project(ps_q, "m", q, q_mm)
                if before:
                    mix_values(g - 1)
                    pe.wait_ge(s_masked, g)
                project(ps_g, "g", q, gate_mm)
                if ahead >= 1:
                    if before:
                        if not (isinstance(g, int) and g == 1):
                            pe.wait_ge(y_done, KD * (g - 1))
                    transpose_tokens(g + 1, 1 - q)
                if before:
                    pe.wait_ge(o_gated, KD * g)
                rows(ps_v, xT_hi[q], xT_lo[q], "v", v_mm)
                if before:
                    pe.wait_ge(o_lo_done, KD * g)
                    if ahead >= 1:
                        pe.wait_ge(xT_lo_done, KD * (g + 2))
                    rows(ps_t, o_hi, o_lo, "o", y_mm)
                pe.wait_ge(gate_done, KD * (g + 1))
                pe.wait_ge(q_lo_done, KD * (g + 1))
                for t in range(GT):
                    cols = slice(t * P, (t + 1) * P)
                    for k in range(KD):
                        mm = three(ps_g[0][:, cols], xT_hi[q][:, k, cols], xT_lo[q][:, k, cols],
                                   qT_hi[:, k, cols], qT_lo[:, k, cols], k == 0, k == KD - 1)
                mm.then_inc(s_mm, 1)

            groups(pe, emit)
            mix_values(NGR - 1)
            pe.wait_ge(o_lo_done, KD * NGR)
            pe.wait_ge(y_done, KD * (NGR - 1))
            rows(ps_t, o_hi, o_lo, "o", y_mm)


def feed_forward(nc, c, tag, prm, x_in, x_out, scratch):
    with ExitStack() as ctx:
        with nc.sbuf_tensor(tag + "slots", [P, KD, E, B, S], F32) as slots:
            route_stage(nc, c, tag + "r_", x_in, slots, scratch["logits"], scratch["xhat"])
            eout = ctx.enter_context(nc.sbuf_tensor(tag + "eout", [P, B, NSC, D], F32, side="right"))
            expert_stage(nc, c, tag + "e_", prm, slots, eout)
        combine_stage(nc, c, tag + "c_", x_in, x_out, scratch["logits"], eout)


def macaron_kernel(nc, prm, out):
    with ExitStack() as ctx:
        al = Scope(nc, ctx, "")
        c = {n: al.sb(n, [P, w]) for n, w in (("ident", P), ("ones", P), ("minus_half", 8), ("dve_carrier", 1), ("pool_carrier", 1),
                                              ("norm_g", D), ("norm_b", D),
                                              ("biases", 2 * E * KF))}
        c["emb_hi"], c["emb_lo"] = al.sb("emb_hi", [P, KD, SL], F32R), al.sb("emb_lo", [P, KD, SL], F32R)
        scratch = {"logits": nc.dram_tensor("logits", (B * NG, P, NSC, GN), F32, kind="Internal").ap(),
                   "xhat": nc.dram_tensor("xhat", (B * NG, P, GT, D), F32, kind="Internal").ap()}
        x_a = nc.dram_tensor("x_after_ffn", (B, T, D), F32, kind="Internal").ap()
        x_b = nc.dram_tensor("x_after_attention", (B, T, D), F32, kind="Internal").ap()
        setup_stage(nc, c, prm)
        feed_forward(nc, c, "f1", prm, prm["x"], x_a, scratch)
        attention_stage(nc, c, "at_", prm, x_a, x_b)
        feed_forward(nc, c, "f2", prm, x_b, out, scratch)


_INS = {"x": "L0_attn_x", "W_q": "L0_attn_W_q", "W_k": "L0_attn_W_k", "W_v": "L0_attn_W_v", "W_g": "L0_attn_W_g",
        "W_o": "L0_attn_W_o", "log_decay": "L0_attn_log_decay", "norm_g": "L0_ffn_norm_g", "norm_b": "L0_ffn_norm_b",
        "slot_g": "L0_ffn_slot_g", "slot_b": "L0_ffn_slot_b", "scale": "L0_ffn_scale",
        "slot_embeds": "L0_ffn_slot_embeds", "Wg": "L0_ffn_Wg", "bg": "L0_ffn_bg", "Wu": "L0_ffn_Wu",
        "bu": "L0_ffn_bu", "Wd": "L0_ffn_Wd", "bd": "L0_ffn_bd"}


def kernel(**inputs):
    import numpy as _np
    import concourse.bacc as _bacc
    from concourse import mybir as _mybir
    from concourse.bass_utils import run_bass_kernel_spmd as _run

    nc = _bacc.Bacc("TRN2", target_bir_lowering=False, num_devices=1)
    arrays, prm = {}, {}
    for short, name in _INS.items():
        a = _np.ascontiguousarray(inputs[name])
        arrays[f"in_{name}"] = a
        prm[short] = nc.dram_tensor(f"in_{name}", a.shape, _mybir.dt.from_np(a.dtype), kind="ExternalInput").ap()
    out = nc.dram_tensor("out", (B, T, D), _mybir.dt.float32, kind="ExternalOutput").ap()
    macaron_kernel(nc, prm, out)
    r = _run(nc, [arrays], core_ids=[0])
    return r.results[0]["out"]
```

```python
from contextlib import ExitStack

import concourse.bass as bass
from concourse import mybir

F32 = mybir.dt.float32
F32R = mybir.dt.float32r
ALU = mybir.AluOpType
ACT = mybir.ActivationFunctionType
AX_X = mybir.AxisListType.X

P = 128
B, T, D = 4, 2048, 256
E, S, F = 16, 64, 512
CHUNK = 32
EPS = 1e-5
KD = D // P
KF = F // P
SL = E * S
NSC = SL // P
GT = 4
GN = GT * P
NG = T // GN
BANK = 512
HB = SL // BANK
DMA = 16


class Scope:

    def __init__(self, nc, ctx, tag):
        self.nc, self.ctx, self.tag, self.sems = nc, ctx, tag, []
        ctx.callback(self.release)

    def sb(self, name, shape, dt=F32):
        return self.ctx.enter_context(self.nc.sbuf_tensor(self.tag + name, shape, dt))

    def ps(self, name, shape):
        return self.ctx.enter_context(self.nc.psum_tensor(self.tag + name, shape, F32))

    def sem(self, name):
        self.sems.append(self.nc.alloc_semaphore(self.tag + name))
        return self.sems[-1]

    def release(self):
        if self.sems:
            self.nc.clear_and_free_semaphores(self.sems)
            self.nc.all_engine_barrier()


def rd(ap):
    return ap.bitcast(F32)


def dve_wait(dve, c, sem, value):
    dve.wait_ge(sem, value)
    dve.memset(c["dve_carrier"][:, :], 0.0)


def pool_wait(pool, c, sem, value, col=0):
    pool.wait_ge(sem, value)
    pool.tensor_tensor(c["pool_carrier"][:, col:col + 1], c["minus_half"][:, 0:1], c["minus_half"][:, 0:1], ALU.add)


def setup_stage(nc, c, prm):
    with ExitStack() as ctx:
        al = Scope(nc, ctx, "su_")
        emb = al.sb("emb", [P, NSC, D])
        slot_g, slot_b, scale = al.sb("slot_g", [P, D]), al.sb("slot_b", [P, D]), al.sb("scale", [P, 1])
        bias_rows = al.sb("bias_rows", [E * KF, 2, P])
        stats, mv = al.sb("stats", [P, NSC, 6]), al.sb("mv", [P, NSC, 2])
        var_eps, rstd = al.sb("var_eps", [P, NSC]), al.sb("rstd", [P, NSC])
        norm_g, norm_b, shifted = al.sb("norm_g", [P, D]), al.sb("norm_b", [P, D]), al.sb("shifted", [P, NSC, D])
        tr = [al.ps(f"tr{i}", [P, BANK]) for i in range(2)]
        loads, const_done, ident_zero = al.sem("loads"), al.sem("const_done"), al.sem("ident_zero")
        stats_done, mv_done, var_done = al.sem("stats_done"), al.sem("mv_done"), al.sem("var_done")
        rstd_done, emb_step, emb_done = al.sem("rstd_done"), al.sem("emb_step"), al.sem("emb_done")
        tr_done, hi_done, lo_done = al.sem("tr_done"), al.sem("hi_done"), al.sem("lo_done")
        bias_tr, bias_done = al.sem("bias_tr"), al.sem("bias_done")
        block = ctx.enter_context(nc.Block())

        LOADS = 8 + 2 * KD

        def row(v):
            return v.rearrange("(a n) -> a n", a=1).to_broadcast([P, v.shape[0]])

        @block.sync
        def _(sp):
            sp.dma_start(emb[:, :, :], prm["slot_embeds"].rearrange("e s d -> (e s) d")
                         .rearrange("(t p) d -> p t d", p=P)).then_inc(loads, DMA)
            sp.dma_start(slot_g[:, :], row(prm["slot_g"])).then_inc(loads, DMA)
            sp.dma_start(slot_b[:, :], row(prm["slot_b"])).then_inc(loads, DMA)
            sp.dma_start(scale[:, :], row(prm["scale"])).then_inc(loads, DMA)
            sp.dma_start(norm_g[:, :], row(prm["norm_g"])).then_inc(loads, DMA)
            sp.dma_start(norm_b[:, :], row(prm["norm_b"])).then_inc(loads, DMA)
            for name, v in (("gain", "norm_g"), ("shift", "norm_b")):
                for k in range(KD):
                    sp.dma_start(c[name][:, k:k + 1], prm[v][k * P:(k + 1) * P].rearrange("(p a) -> p a", a=1))\
                      .then_inc(loads, DMA)
            for i, name in enumerate(("bg", "bu")):
                sp.dma_start(bias_rows[:, i, :], prm[name].rearrange("e (c p) -> (e c) p", p=P)).then_inc(loads, DMA)
            sp.wait_ge(loads, LOADS * DMA)

        @block.gpsimd
        def _(pool):
            pool.memset(c["ones"][:, :], 1.0).then_inc(const_done, 1)
            pool.memset(c["minus_half"][:, :], -0.5).then_inc(const_done, 1)
            pool.memset(c["ident"][:, :], 0.0).then_inc(ident_zero, 1)
            pool.wait_ge(ident_zero, 1)
            pool.affine_select(out=c["ident"][:, :], in_=c["ident"][:, :], compare_op=ALU.not_equal, fill=1.0,
                               base=0, pattern=[[-1, P]], channel_multiplier=1).then_inc(const_done, 1)
            pool.wait_ge(mv_done, NSC)
            pool.tensor_scalar(var_eps[:, :], mv[:, :, 1], 1.0, EPS, ALU.mult, ALU.add).then_inc(var_done, 1)
            pool.wait_ge(var_done, 1)
            pool.wait_ge(const_done, 3)
            pool.tensor_tensor(rstd[:, :], var_eps[:, :], c["minus_half"][:, 0:NSC], ALU.pow).then_inc(rstd_done, 1)

        @block.vector
        def _(dve):
            dve.wait_ge(loads, LOADS * DMA)
            for t in range(NSC):
                dve.bn_stats(stats[:, t, :], emb[:, t, :]).then_inc(stats_done, 1)
            for t in range(NSC):
                dve.wait_ge(stats_done, t + 1)
                dve.bn_aggr(mv[:, t, :], stats[:, t, :]).then_inc(mv_done, 1)
            dve.wait_ge(rstd_done, 1)
            dve.wait_ge(mv_done, NSC)
            for t in range(NSC):
                dve.tensor_scalar(emb[:, t, :], emb[:, t, :], mv[:, t, 0:1], rstd[:, t:t + 1],
                                  ALU.subtract, ALU.mult).then_inc(emb_step, 1)
            dve.wait_ge(emb_step, NSC)
            dve.tensor_tensor(emb[:, :, :], emb[:, :, :], slot_g[:, :].unsqueeze(1).to_broadcast([P, NSC, D]),
                              ALU.mult).then_inc(emb_step, 1)
            dve.wait_ge(emb_step, NSC + 1)
            dve.tensor_tensor(emb[:, :, :], emb[:, :, :], slot_b[:, :].unsqueeze(1).to_broadcast([P, NSC, D]),
                              ALU.add).then_inc(emb_step, 1)
            dve.wait_ge(emb_step, NSC + 2)
            dve.tensor_scalar(emb[:, :, :], emb[:, :, :], scale[:, 0:1], None, ALU.mult).then_inc(emb_step, 1)
            dve.wait_ge(emb_step, NSC + 3)
            dve.tensor_tensor(shifted[:, :, :], emb[:, :, :], norm_b[:, :].unsqueeze(1).to_broadcast([P, NSC, D]),
                              ALU.mult).then_inc(emb_step, 1)
            dve.tensor_tensor(emb[:, :, :], emb[:, :, :], norm_g[:, :].unsqueeze(1).to_broadcast([P, NSC, D]),
                              ALU.mult).then_inc(emb_done, 1)
            dve.wait_ge(emb_step, NSC + 4)
            dve.tensor_reduce(c["slot_shift"][:, :], shifted[:, :, :], AX_X, ALU.add).then_inc(emb_step, 1)
            for n in range(KD * HB):
                k, h = n // HB, n % HB
                dve.wait_ge(hi_done, n + 1)
                dve.tensor_tensor(c["emb_lo"][:, k, h * BANK:(h + 1) * BANK], tr[n % 2][:, :],
                                  rd(c["emb_hi"][:, k, h * BANK:(h + 1) * BANK]), ALU.subtract).then_inc(lo_done, 1)

        @block.tensor
        def _(pe):
            pe.wait_ge(const_done, 3)
            pe.wait_ge(emb_done, 1)
            for n in range(KD * HB):
                k, h = n // HB, n % HB
                if n >= 2:
                    pe.wait_ge(lo_done, n - 1)
                for j in range(BANK // P):
                    mm = pe.transpose(tr[n % 2][:, j * P:(j + 1) * P], emb[:, h * (BANK // P) + j, k * P:(k + 1) * P],
                                      c["ident"][:, :])
                mm.then_inc(tr_done, 1)
            pe.wait_ge(lo_done, KD * HB)
            for i in range(2):
                mm = pe.transpose(tr[0][:, i * E * KF:(i + 1) * E * KF], bias_rows[:, i, :],
                                  c["ident"][0:E * KF, 0:E * KF])
            mm.then_inc(bias_tr, 1)

        @block.scalar
        def _(act):
            for n in range(KD * HB):
                k, h = n // HB, n % HB
                act.wait_ge(tr_done, n + 1)
                act.activation(c["emb_hi"][:, k, h * BANK:(h + 1) * BANK], tr[n % 2][:, :], ACT.Copy).then_inc(hi_done, 1)
            act.wait_ge(bias_tr, 1)
            act.activation(c["biases"][:, :], tr[0][:, 0:2 * E * KF], ACT.Copy).then_inc(bias_done, 1)


def route_stage(nc, c, tag, x_in, slots, neg_row_max, logits_dram, xn_dram):
    with ExitStack() as ctx:
        al = Scope(nc, ctx, tag)
        lt = al.sb("lt", [P, NG, NSC, GN])
        et = al.sb("et", [P, NSC, GN])
        xin = [al.sb(f"xin{i}", [P, GT, D]) for i in range(2)]
        over_chunks = al.sb("over_chunks", [P, GN])
        xT_hi = [al.sb(f"xT_hi{i}", [P, KD, GN], F32R) for i in range(2)]
        xT_lo = [al.sb(f"xT_lo{i}", [P, KD, GN], F32R) for i in range(2)]
        xback = [al.sb(f"xback{i}", [P, GT, D]) for i in range(2)]
        xs_hi = [al.sb(f"xs_hi{i}", [P, D], F32R) for i in range(2)]
        xs_lo = [al.sb(f"xs_lo{i}", [P, D], F32R) for i in range(2)]
        e_hi = [al.sb(f"e_hi{i}", [P, SL], F32R) for i in range(2)]
        e_lo = [al.sb(f"e_lo{i}", [P, SL], F32R) for i in range(2)]
        diag, inv_rows = al.sb("diag", [P, NSC, P]), al.sb("inv_rows", [P, SL])
        stats, mv = [al.sb(f"stats{i}", [P, GT, 6]) for i in range(2)], [al.sb(f"mv{i}", [P, GT, 2]) for i in range(2)]
        var_eps, rstd = [al.sb(f"var_eps{i}", [P, GT]) for i in range(2)], [al.sb(f"rstd{i}", [P, GT]) for i in range(2)]
        gmax, neg_max = al.sb("gmax", [P, NSC, NG]), al.sb("neg_max", [P, NSC])
        gsum, tsum, inv = al.sb("gsum", [P, NSC, NG]), al.sb("tsum", [P, NSC]), al.sb("inv", [P, NSC])

        ps_l = [al.ps(f"ps_l{i}", [P, BANK]) for i in range(2)]
        ps_t = [al.ps(f"ps_t{i}", [P, BANK]) for i in range(HB)]
        ps_s = [al.ps(f"ps_s{i}", [P, BANK]) for i in range(KD * HB)]

        x_loaded = [al.sem(f"x_loaded{i}") for i in range(2)]
        xn_stored = [al.sem(f"xn_stored{i}") for i in range(2)]
        xback_loaded = [al.sem(f"xback_loaded{i}") for i in range(2)]
        lt_stored = [al.sem(f"lt_stored{g}") for g in range(NG)]
        stats_done, mv_done, var_done, rstd_done = (al.sem(n) for n in ("stats_done", "mv_done", "var_done", "rstd_done"))
        xn_done, chunk_max, row_tr, row_max_done = (al.sem(n) for n in ("xn_done", "chunk_max", "row_tr", "row_max_done"))
        scaled, slots_done = al.sem("scaled"), al.sem("slots_done")
        xT_tr, xT_hi_done, xT_lo_done = (al.sem(n) for n in ("xT_tr", "xT_hi_done", "xT_lo_done"))
        logit_mm, logit_out, max_done = (al.sem(n) for n in ("logit_mm", "logit_out", "max_done"))
        exp_done, e_tr, e_hi_done, e_lo_done = (al.sem(n) for n in ("exp_done", "e_tr", "e_hi_done", "e_lo_done"))
        xs_hi_done, xs_done, dispatched = (al.sem(n) for n in ("xs_hi_done", "xs_done", "dispatched"))
        tsum_done, inv_done, diag_done = (al.sem(n) for n in ("tsum_done", "inv_done", "diag_done"))
        inv_mm, inv_out = al.sem("inv_mm"), al.sem("inv_out")
        block = ctx.enter_context(nc.Block())

        LAST = B * NG - 1

        def batches(eng, emit):
            emit(0, True, False)
            with eng.Fori(1, B - 1) as b:
                emit(b, True, True)
            emit(B - 1, True, True)
            emit(B, False, True)

        def exp_of(g, fill):
            return et if fill else lt[:, g, :, :]

        def exists(b, g, ahead):
            return not isinstance(b, int) or b * NG + g + ahead <= LAST

        @block.sync
        def _(sp):
            x_g = x_in.rearrange("b (g p t) d -> (b g) p t d", g=NG, t=GT)

            def load_x(i, par):
                sp.dma_start(xin[par][:, :, :], x_g[i]).then_inc(x_loaded[par], DMA)

            def store_xn(i, par):
                sp.wait_ge(xn_done, i + 1)
                sp.dma_start(xn_dram[i], xin[par][:, :, :]).then_inc(xn_stored[par], DMA)

            def load_back(i, par):
                sp.wait_ge(xs_done, 1 + GT * (i - NG))
                sp.wait_ge(xn_stored[par], DMA * ((i + 1 - NG) // 2 + 1))
                sp.dma_start(xback[par][:, :, :], xn_dram[i + 1 - NG]).then_inc(xback_loaded[par], DMA)

            load_x(0, 0)
            load_x(1, 1)
            store_xn(0, 0)
            sp.wait_ge(xT_tr, KD)
            sp.wait_ge(xn_stored[0], DMA)
            load_x(2, 0)
            store_xn(1, 1)

            def emit(b, fill, drain):
                for g in range(NG):
                    i = b * NG + g
                    par = (g + 1) % 2
                    if drain and (fill or g < NG - 1):
                        load_back(i, par)
                    if fill and not drain and g == NG - 1:
                        sp.wait_ge(xn_stored[0], DMA)
                        sp.dma_start(xback[0][:, :, :], xn_dram[0]).then_inc(xback_loaded[0], DMA)
                    if fill and exists(b, g, 3):
                        sp.wait_ge(xT_tr, KD * (i + 2))
                        sp.wait_ge(xn_stored[par], DMA * ((i + 1) // 2 + 1))
                        load_x(i + 3, par)
                    if fill and exists(b, g, 2):
                        store_xn(i + 2, g % 2)
                    if fill:
                        sp.wait_ge(logit_out, NSC * (i + 1))
                        sp.dma_start(logits_dram[i], lt[:, g, :, :]).then_inc(lt_stored[g], DMA)

            batches(sp, emit)
            for s in lt_stored:
                sp.wait_ge(s, B * DMA)
            for s in xn_stored:
                sp.wait_ge(s, B * NG // 2 * DMA)

        @block.gpsimd
        def _(pool):
            def norm_scale(i, par):
                pool_wait(pool, c, mv_done, GT * (i + 1))
                pool.tensor_scalar(var_eps[par][:, :], mv[par][:, :, 1], 1.0 + EPS, EPS * EPS,
                                   ALU.mult, ALU.add).then_inc(var_done, 1)
                pool.wait_ge(var_done, i + 1)
                pool.tensor_tensor(rstd[par][:, :], var_eps[par][:, :], c["minus_half"][:, 0:GT],
                                   ALU.pow).then_inc(rstd_done, 1)

            def normalize(i, par):
                pool_wait(pool, c, rstd_done, i + 1, 1)
                for t in range(GT):
                    last = pool.tensor_scalar(xin[par][:, t, :], xin[par][:, t, :], mv[par][:, t, 0:1],
                                              rstd[par][:, t:t + 1], ALU.subtract, ALU.mult)
                last.then_inc(xn_done, 1)

            norm_scale(0, 0)
            norm_scale(1, 1)

            def emit(b, fill, drain):
                for g in range(NG):
                    if fill and exists(b, g, 2):
                        norm_scale(b * NG + g + 2, g % 2)
                        normalize(b * NG + g + 2, g % 2)

            batches(pool, emit)

        @block.vector
        def _(dve):
            for s in (xs_done, tsum_done, scaled, e_lo_done):
                dve.sem_inc(s, 1)

            def token_stats(i, par):
                dve.wait_ge(x_loaded[par], DMA * (i // 2 + 1))
                for t in range(GT):
                    dve.bn_stats(stats[par][:, t, :], xin[par][:, t, :]).then_inc(stats_done, 1)
                dve_wait(dve, c, stats_done, GT * (i + 1))
                for t in range(GT):
                    dve.bn_aggr(mv[par][:, t, :], stats[par][:, t, :]).then_inc(mv_done, 1)

            def transposed_lo(i, par, k):
                dve.wait_ge(xT_hi_done, KD * i + k + 1)
                dve.tensor_tensor(xT_lo[par][:, k, :], ps_t[k][:, :], rd(xT_hi[par][:, k, :]),
                                  ALU.subtract).then_inc(xT_lo_done, 1)

            def logits_out(b, g, i, sc, drain):
                dve.wait_ge(logit_mm, NSC * i + sc + 1)
                if drain:
                    dve.wait_ge(exp_done, NSC * (i - NG) + sc + 1)
                    dve.wait_ge(lt_stored[g], DMA * b)
                dve.tensor_scalar(lt[:, g, sc, :], ps_l[sc % 2][:, :], c["slot_shift"][:, sc:sc + 1], None, ALU.add,
                                  ALU.max, accum_out=gmax[:, sc, g:g + 1]).then_inc(logit_out, 1)

            def over_chunks_max(g, i, sc):
                dve.wait_ge(logit_out, NSC * i + sc + 1)
                if sc == 1:
                    dve.wait_ge(row_tr, 1 + i)
                else:
                    dve.wait_ge(chunk_max, (NSC - 1) * i + sc - 1)
                dve.tensor_tensor(over_chunks[:, :], lt[:, g, 0, :] if sc == 1 else over_chunks[:, :], lt[:, g, sc, :],
                                  ALU.max).then_inc(chunk_max, 1)

            def row_max(g, b, i):
                dve.wait_ge(row_tr, 2 + i)
                dve.tensor_reduce(neg_row_max[:, b, g, :], ps_t[0][:, :].rearrange("p (t s) -> p t s", s=P), AX_X,
                                  ALU.max, negate=True).then_inc(row_max_done, 1)

            def token_parts(j, par, t):
                dve.wait_ge(xs_hi_done, GT * j + t + 1)
                dve.tensor_tensor(xs_lo[t % 2][:, :], xback[par][:, t, :], rd(xs_hi[t % 2][:, :]),
                                  ALU.subtract).then_inc(xs_done, 1)

            def exp_lo(j, t, h):
                n = HB * (GT * j + t) + h
                dve.wait_ge(e_hi_done, n + 1)
                dve.tensor_tensor(e_lo[t % 2][:, h * BANK:(h + 1) * BANK], ps_t[h][:, :],
                                  rd(e_hi[t % 2][:, h * BANK:(h + 1) * BANK]), ALU.subtract).then_inc(e_lo_done, 1)

            def normalize(i):
                dve.wait_ge(rstd_done, i + 1)
                dve.wait_ge(mv_done, GT * (i + 1))
                for t in range(GT):
                    last = dve.tensor_scalar(xin[i][:, t, :], xin[i][:, t, :], mv[i][:, t, 0:1],
                                             rstd[i][:, t:t + 1], ALU.subtract, ALU.mult)
                last.then_inc(xn_done, 1)

            token_stats(0, 0)
            token_stats(1, 1)
            normalize(0)
            normalize(1)
            for k in range(KD):
                transposed_lo(0, 0, k)

            def emit(b, fill, drain):
                for g in range(NG):
                    i = b * NG + g
                    j = i - NG

                    def out(sc):
                        if fill:
                            logits_out(b, g, i, sc, drain)
                            if sc >= 2:
                                over_chunks_max(g, i, sc - 1)

                    nxt = fill and exists(b, g, 1)
                    nxt2 = fill and exists(b, g, 2)
                    def tile(t):
                        if drain:
                            exp_lo(j, t, 0)
                            exp_lo(j, t, 1)
                            token_parts(j, g % 2, t)

                    out(0)
                    if nxt:
                        transposed_lo(i + 1, (g + 1) % 2, 0)
                        transposed_lo(i + 1, (g + 1) % 2, 1)
                    out(1)
                    out(2)
                    if nxt2:
                        token_stats(i + 2, g % 2)
                    tile(0)
                    out(3)
                    out(4)
                    tile(1)
                    if drain and g == NG - 1:
                        dve.wait_ge(exp_done, NSC * (j + 1))
                        dve.tensor_reduce(tsum[:, :], gsum[:, :, :], AX_X, ALU.add).then_inc(tsum_done, 1)
                        dve.wait_ge(tsum_done, 1 + b)
                        dve.reciprocal(inv[:, :], tsum[:, :]).then_inc(inv_done, 1)
                        dve.wait_ge(inv_done, b)
                        dve.wait_ge(inv_mm, 1 + HB * (b - 1))
                        dve.tensor_tensor(diag[:, :, :], c["ident"][:, :].unsqueeze(1).to_broadcast([P, NSC, P]),
                                          inv[:, :].unsqueeze(2).to_broadcast([P, NSC, P]),
                                          ALU.mult).then_inc(diag_done, 1)
                    out(5)
                    tile(2)
                    out(6)
                    tile(3)
                    out(7)
                    if fill:
                        over_chunks_max(g, i, NSC - 1)
                        if g == NG - 1:
                            dve.wait_ge(logit_out, NSC * (i + 1))
                            if drain:
                                dve.wait_ge(exp_done, NSC * (j + 1))
                            dve.tensor_reduce(neg_max[:, :], gmax[:, :, :], AX_X, ALU.max, negate=True)\
                               .then_inc(max_done, 1)
                        row_max(g, b, i)
                    if drain:
                        if g == NG - 1:
                            dve.wait_ge(dispatched, 1 + GT * (j + 1))
                            dve.wait_ge(inv_out, 1 + HB * b)
                            for k in range(KD):
                                for h in range(HB):
                                    dve.tensor_tensor(
                                        slots[:, k, h * (E // HB):(h + 1) * (E // HB), b - 1, :],
                                        ps_s[k * HB + h][:, :].rearrange("p (e s) -> p e s", s=S),
                                        inv_rows[:, h * BANK:(h + 1) * BANK].rearrange("p (e s) -> p e s", s=S),
                                        ALU.mult).then_inc(scaled, 1)

            batches(dve, emit)

        @block.scalar
        def _(act):
            def transposed_hi(i, par, k):
                act.wait_ge(xT_tr, KD * i + k + 1)
                act.activation(xT_hi[par][:, k, :], ps_t[k][:, :], ACT.Copy).then_inc(xT_hi_done, 1)

            def exponentials(g, fill, chunks):
                for sc in chunks:
                    act.activation(exp_of(g, fill)[:, sc, :], lt[:, g, sc, :], ACT.Exp, bias=neg_max[:, sc:sc + 1],
                                   accum_out=gsum[:, sc, g:g + 1]).then_inc(exp_done, 1)

            act.sem_inc(inv_out, 1)
            for k in range(KD):
                transposed_hi(0, 0, k)

            def emit(b, fill, drain):
                for g in range(NG):
                    i = b * NG + g
                    j = i - NG
                    if drain and fill and g > 0:
                        act.wait_ge(e_tr, 1 + HB * GT * j)
                        exponentials(g, True, range(NSC))
                    if fill and exists(b, g, 1):
                        for k in range(KD):
                            transposed_hi(i + 1, (g + 1) % 2, k)
                    if drain:
                        for t in range(GT):
                            if t == 0:
                                act.wait_ge(xback_loaded[g % 2], DMA * (j // 2 + 1))
                            act.wait_ge(dispatched, 1 + GT * j + max(t - 1, 0))
                            act.activation(xs_hi[t % 2][:, :], xback[g % 2][:, t, :], ACT.Copy).then_inc(xs_hi_done, 1)
                            for h in range(HB):
                                act.wait_ge(e_tr, 1 + HB * (GT * j + t) + h + 1)
                                act.activation(e_hi[t % 2][:, h * BANK:(h + 1) * BANK], ps_t[h][:, :],
                                               ACT.Copy).then_inc(e_hi_done, 1)
                            if not fill and g < NG - 1:
                                if t == 0:
                                    act.wait_ge(lt_stored[g + 1], DMA * B)
                                exponentials(g + 1, False, range(3 * t, min(3 * t + 3, NSC)))
                        if g == NG - 1:
                            act.wait_ge(scaled, 1 + KD * HB * (b - 1))
                            for h in range(HB):
                                act.wait_ge(inv_mm, 1 + HB * (b - 1) + h + 1)
                                act.activation(inv_rows[:, h * BANK:(h + 1) * BANK], ps_t[h][:, :],
                                               ACT.Copy).then_inc(inv_out, 1)
                    if fill and g == NG - 1:
                        act.wait_ge(max_done, b + 1)
                        act.wait_ge(tsum_done, 1 + b)
                        act.wait_ge(e_tr, 1 + HB * GT * b * NG)
                        more = exists(b, g, 1)
                        if not more:
                            act.wait_ge(lt_stored[0], DMA * B)
                        exponentials(0, more, range(NSC))
                    if drain and g == NG - 1:
                        for k in range(KD):
                            for h in range(HB):
                                act.wait_ge(scaled, 1 + KD * HB * (b - 1) + HB * k + h + 1)
                                half = slots[:, k, h * (E // HB):(h + 1) * (E // HB), b - 1, :]
                                act.activation(half, half, ACT.Identity, bias=c["shift"][:, k:k + 1],
                                               scale=c["gain"][:, k:k + 1]).then_inc(slots_done, 1)

            batches(act, emit)

        @block.tensor
        def _(pe):
            def transpose_tokens(i, par):
                pe.wait_ge(xn_done, i + 1)
                for k in range(KD):
                    for t in range(GT):
                        mm = pe.transpose(ps_t[k][:, t * P:(t + 1) * P], xin[par][:, t, k * P:(k + 1) * P],
                                          c["ident"][:, :])
                    mm.then_inc(xT_tr, 1)

            def logits(i, par, sc, start_of_phase):
                if sc == 0:
                    pe.wait_ge(xT_lo_done, KD * (i + 1))
                if not (start_of_phase and sc < 2):
                    pe.wait_ge(logit_out, NSC * i + sc - 1)
                cols = slice(sc * P, (sc + 1) * P)
                for k in range(KD):
                    pe.matmul(ps_l[sc % 2][:, :], c["emb_hi"][:, k, cols], xT_hi[par][:, k, :], start=k == 0, stop=False)
                    pe.matmul(ps_l[sc % 2][:, :], c["emb_hi"][:, k, cols], xT_lo[par][:, k, :], start=False, stop=False)
                    mm = pe.matmul(ps_l[sc % 2][:, :], c["emb_lo"][:, k, cols], xT_hi[par][:, k, :],
                                   start=False, stop=k == KD - 1)
                mm.then_inc(logit_mm, 1)

            def transpose_row_max(i):
                pe.wait_ge(chunk_max, (NSC - 1) * (i + 1))
                for t in range(GT):
                    mm = pe.transpose(ps_t[0][:, t * P:(t + 1) * P], over_chunks[:, t * P:(t + 1) * P], c["ident"][:, :])
                mm.then_inc(row_tr, 1)

            def transpose_exp(j, g, t, fill):
                for h in range(HB):
                    for n in range(BANK // P):
                        mm = pe.transpose(ps_t[h][:, n * P:(n + 1) * P],
                                          exp_of(g, fill)[:, h * (BANK // P) + n, t * P:(t + 1) * P], c["ident"][:, :])
                    mm.then_inc(e_tr, 1)

            def dispatch(b, g, j, t):
                start = g == 0 and t == 0
                if start:
                    pe.wait_ge(scaled, 1 + KD * HB * (b - 1))
                pe.wait_ge(xs_done, 1 + GT * j + t + 1)
                pe.wait_ge(e_lo_done, 1 + HB * (GT * j + t + 1))
                stop = g == NG - 1 and t == GT - 1
                for k in range(KD):
                    cols = slice(k * P, (k + 1) * P)
                    for h in range(HB):
                        half = slice(h * BANK, (h + 1) * BANK)
                        pe.matmul(ps_s[k * HB + h][:, :], xs_hi[t % 2][:, cols], e_hi[t % 2][:, half], start=start, stop=False)
                        pe.matmul(ps_s[k * HB + h][:, :], xs_hi[t % 2][:, cols], e_lo[t % 2][:, half], start=False, stop=False)
                    for h in range(HB):
                        half = slice(h * BANK, (h + 1) * BANK)
                        mm = pe.matmul(ps_s[k * HB + h][:, :], xs_lo[t % 2][:, cols], e_hi[t % 2][:, half],
                                       start=False, stop=stop)
                mm.then_inc(dispatched, 1)

            for s in (dispatched, inv_mm, e_tr, row_tr):
                pe.sem_inc(s, 1)
            transpose_tokens(0, 0)

            def emit(b, fill, drain):
                for g in range(NG):
                    i = b * NG + g
                    j = i - NG
                    begin = isinstance(b, int) and b == 0 and g == 0
                    mm = (lambda sc: logits(i, g % 2, sc, begin)) if fill else (lambda sc: None)
                    nxt = fill and exists(b, g, 1)
                    mm(0)
                    if nxt:
                        pe.wait_ge(xT_lo_done, KD * (i + 1))
                        if not begin:
                            pe.wait_ge(row_max_done, i)
                        if drain:
                            pe.wait_ge(e_lo_done, 1 + HB * GT * j)
                            if g == 0:
                                pe.wait_ge(inv_out, 1 + HB * (b - 1))
                        transpose_tokens(i + 1, (g + 1) % 2)
                    mm(1)
                    mm(2)
                    if drain and (fill or g == 0):
                        pe.wait_ge(exp_done, NSC * (j + 1))
                        if nxt:
                            pe.wait_ge(xT_lo_done, KD * (i + 2))
                        else:
                            pe.wait_ge(row_max_done, min(i, LAST + 1))
                            pe.wait_ge(e_lo_done, 1 + HB * GT * j)
                            if g == 0:
                                pe.wait_ge(inv_out, 1 + HB * (b - 1))
                        transpose_exp(j, g, 0, fill)
                    mm(3)
                    mm(4)
                    for t in range(GT):
                        if drain:
                            pe.wait_ge(e_lo_done, 1 + HB * (GT * j + t + 1))
                            if t < GT - 1:
                                transpose_exp(j, g, t + 1, fill)
                            elif g == NG - 1:
                                pe.wait_ge(diag_done, b)
                                for h in range(HB):
                                    pe.matmul(ps_t[h][:, :], c["ones"][:, :],
                                              diag[:, h * (BANK // P):(h + 1) * (BANK // P), :],
                                              start=True, stop=True).then_inc(inv_mm, 1)
                            elif not fill:
                                pe.wait_ge(exp_done, NSC * (j + 2))
                                transpose_exp(j + 1, g + 1, 0, False)
                            dispatch(b, g, j, t)
                        if t < NSC - 5:
                            mm(5 + t)
                    if fill:
                        if nxt:
                            pe.wait_ge(xT_lo_done, KD * (i + 2))
                        if drain and g == NG - 1:
                            pe.wait_ge(inv_out, 1 + HB * b)
                        transpose_row_max(i)

            batches(pe, emit)


def expert_stage(nc, c, tag, prm, slots, eout):
    with ExitStack() as ctx:
        al = Scope(nc, ctx, tag)
        raw = {n: [al.sb(f"raw_{n}{q}", [P, *shape]) for q in range(2)]
               for n, shape in (("g", (KD, F)), ("u", (KD, F)), ("d", (KF, D)))}
        hi = {n: [al.sb(f"hi_{n}{q}", [P, *shape], F32R) for q in range(2)]
              for n, shape in (("g", (KD, F)), ("u", (KD, F)), ("d", (KF, D)))}
        lo = {n: [al.sb(f"lo_{n}{q}", [P, *shape], F32R) for q in range(2)]
              for n, shape in (("g", (KD, F)), ("u", (KD, F)), ("d", (KF, D)))}
        bd = [al.sb(f"bd{q}", [P, D]) for q in range(2)]
        R = B * S
        in_hi = [al.sb(f"in_hi{q}", [P, KD, R], F32R) for q in range(2)]
        in_lo = [al.sb(f"in_lo{q}", [P, KD, R], F32R) for q in range(2)]
        gel = [al.sb(f"gel{q}", [P, KF, R]) for q in range(2)]
        h_hi = [al.sb(f"h_hi{q}", [P, KF, R], F32R) for q in range(2)]
        h_lo = [al.sb(f"h_lo{q}", [P, KF, R], F32R) for q in range(2)]
        ps_h = [al.ps(f"ps_h{f}", [P, BANK]) for f in range(KF)]
        ps_o = [al.ps(f"ps_o{q}", [P, BANK]) for q in range(2)]
        gate_up_loaded = [al.sem(f"gate_up_loaded{q}") for q in range(2)]
        down_loaded = [al.sem(f"down_loaded{q}") for q in range(2)]
        bd_loaded = [al.sem(f"bd_loaded{q}") for q in range(2)]
        names = ("gate_up_hi", "gate_lo", "up_lo", "down_hi", "down_lo", "in_hi_done", "in_lo_done", "hidden_mm",
                 "gelu_done", "hidden_out", "h_hi_done", "h_lo_done", "down_mm", "eout_done")
        (gate_up_hi, gate_lo, up_lo, down_hi, down_lo, in_hi_done, in_lo_done, hidden_mm,
         gelu_done, hidden_out, h_hi_done, h_lo_done, down_mm, eout_done) = (al.sem(n) for n in names)
        block = ctx.enter_context(nc.Block())
        w_src = {"g": prm["Wg"].rearrange("e (k p) f -> e p k f", p=P), "u": prm["Wu"].rearrange("e (k p) f -> e p k f", p=P),
                 "d": prm["Wd"].rearrange("e (k p) o -> e p k o", p=P)}

        def pairs(eng, emit):
            emit(0, True)
            with eng.Fori(1, E // 2) as pair:
                emit(pair, False)

        @block.sync
        def _(sp):
            def load_bias(e, q, first):
                if not first:
                    sp.wait_ge(eout_done, 1 + B * (e - 1))
                sp.dma_start(bd[q][:, :], prm["bd"][e].rearrange("(a n) -> a n", a=1).to_broadcast([P, D]))\
                  .then_inc(bd_loaded[q], DMA)

            def emit(pair, first):
                for q in range(2):
                    e = 2 * pair + q
                    if not first:
                        sp.wait_ge(gate_lo, e - 1)
                        sp.wait_ge(up_lo, e - 1)
                        sp.wait_ge(down_lo, e - 1)
                    for n in "gu":
                        sp.dma_start(raw[n][q][:, :, :], w_src[n][e]).then_inc(gate_up_loaded[q], DMA)
                    sp.dma_start(raw["d"][q][:, :, :], w_src["d"][e]).then_inc(down_loaded[q], DMA)
                    if not first:
                        load_bias(e - 2, q, isinstance(pair, int) and pair == 1)

            emit(0, True)
            emit(1, False)
            with sp.Fori(2, E // 2) as pair:
                emit(pair, False)
            for q in range(2):
                load_bias(E - 2 + q, q, False)

        @block.gpsimd
        def _(pool):
            def emit(pair, first):
                for q in range(2):
                    e = 2 * pair + q
                    pool.wait_ge(gate_up_hi, 2 * (e + 1))
                    pool.tensor_tensor(lo["u"][q][:, :, :], raw["u"][q][:, :, :], rd(hi["u"][q][:, :, :]),
                                       ALU.subtract).then_inc(up_lo, 1)
                    if not first:
                        pool.wait_ge(down_mm, e - 1)
                    pool_wait(pool, c, down_loaded[q], DMA * (pair + 1))
                    pool.tensor_scalar(hi["d"][q][:, :, :], raw["d"][q][:, :, :], 1.0, 0.0, ALU.mult, ALU.add).then_inc(down_hi, 1)
                    pool.wait_ge(down_hi, e + 1)
                    pool.tensor_tensor(lo["d"][q][:, :, :], raw["d"][q][:, :, :], rd(hi["d"][q][:, :, :]),
                                       ALU.subtract).then_inc(down_lo, 1)

            pairs(pool, emit)

        @block.scalar
        def _(act):
            def weights_hi(e, pair, q, first):
                act.wait_ge(gate_up_loaded[q], 2 * DMA * (pair + 1))
                if not first:
                    act.wait_ge(hidden_mm, KF * (e - 1))
                for n in "gu":
                    act.activation(hi[n][q][:, :, :], raw[n][q][:, :, :], ACT.Copy).then_inc(gate_up_hi, 1)
                act.activation(in_hi[q][:, :, :].rearrange("p k (b s) -> p k b s", s=S), slots[:, :, e, :, :],
                               ACT.Copy).then_inc(in_hi_done, 1)

            weights_hi(0, 0, 0, True)

            def emit(pair, first, last):
                for q in range(2):
                    e = 2 * pair + q
                    if not (last and q == 1):
                        weights_hi(e + 1, pair + q, 1 - q, first and q == 0)
                    for f in range(KF):
                        act.wait_ge(hidden_mm, KF * e + f + 1)
                        if f == 0 and not first:
                            act.wait_ge(h_lo_done, e - 1)
                        act.activation(gel[q][:, f, :], ps_h[f][:, 0:R], ACT.Gelu,
                                       bias=c["biases"][:, bass.ds(e * KF + f, 1)]).then_inc(gelu_done, 1)
                    act.wait_ge(hidden_out, KF * (e + 1))
                    if not first:
                        act.wait_ge(down_mm, e - 1)
                    act.activation(h_hi[q][:, :, :], gel[q][:, :, :], ACT.Copy).then_inc(h_hi_done, 1)

            emit(0, True, False)
            with act.Fori(1, E // 2 - 1) as pair:
                emit(pair, False, False)
            emit(E // 2 - 1, False, True)

        @block.vector
        def _(dve):
            def parts_lo(e, q):
                dve.wait_ge(gate_up_hi, 2 * e + 1)
                dve.tensor_tensor(lo["g"][q][:, :, :], raw["g"][q][:, :, :], rd(hi["g"][q][:, :, :]),
                                  ALU.subtract).then_inc(gate_lo, 1)
                dve.wait_ge(in_hi_done, e + 1)
                for k in range(KD):
                    last = dve.tensor_tensor(in_lo[q][:, k, :].rearrange("p (b s) -> p b s", s=S), slots[:, k, e, :, :],
                                             rd(in_hi[q][:, k, :]).rearrange("p (b s) -> p b s", s=S), ALU.subtract)
                last.then_inc(in_lo_done, 1)

            def rows_out(e, pair, q):
                dve.wait_ge(down_mm, e + 1)
                dve.wait_ge(bd_loaded[q], DMA * (pair + 1))
                for b in range(B):
                    half = slice((b % 2) * S, (b % 2) * S + S)
                    dve.tensor_tensor(eout[q * S:(q + 1) * S, b, pair, :], ps_o[q][half, (b // 2) * D:(b // 2 + 1) * D],
                                      bd[q][half, :], ALU.add).then_inc(eout_done, 1)

            dve.sem_inc(eout_done, 1)
            parts_lo(0, 0)

            def emit(pair, first, last):
                for q in range(2):
                    e = 2 * pair + q
                    if not (last and q == 1):
                        parts_lo(e + 1, 1 - q)
                    for f in range(KF):
                        dve.wait_ge(gelu_done, KF * e + f + 1)
                        dve.scalar_tensor_tensor(out=gel[q][:, f, :], in0=ps_h[f][:, R:2 * R],
                                                 scalar=c["biases"][:, bass.ds(E * KF + e * KF + f, 1)],
                                                 in1=gel[q][:, f, :], op0=ALU.add, op1=ALU.mult).then_inc(hidden_out, 1)
                    dve.wait_ge(h_hi_done, e + 1)
                    dve.tensor_tensor(h_lo[q][:, :, :], gel[q][:, :, :], rd(h_hi[q][:, :, :]), ALU.subtract).then_inc(h_lo_done, 1)
                    if not (first and q == 0):
                        rows_out(e - 1, pair - 1 + q, 1 - q)

            emit(0, True, False)
            with dve.Fori(1, E // 2 - 1) as pair:
                emit(pair, False, False)
            emit(E // 2 - 1, False, True)
            rows_out(E - 1, E // 2 - 1, 1)

        @block.tensor
        def _(pe):
            def hidden(e, q, first):
                pe.wait_ge(gate_lo, e + 1)
                pe.wait_ge(up_lo, e + 1)
                pe.wait_ge(in_lo_done, e + 1)
                for f in range(KF):
                    if not (first and q == 0):
                        pe.wait_ge(hidden_out, KF * (e - 1) + f + 1)
                    cols = slice(f * P, (f + 1) * P)
                    for i, n in enumerate("gu"):
                        out = ps_h[f][:, i * R:(i + 1) * R]
                        for k in range(KD):
                            pe.matmul(out, hi[n][q][:, k, cols], in_hi[q][:, k, :], start=k == 0, stop=False)
                            pe.matmul(out, hi[n][q][:, k, cols], in_lo[q][:, k, :], start=False, stop=False)
                            mm = pe.matmul(out, lo[n][q][:, k, cols], in_hi[q][:, k, :], start=False, stop=k == KD - 1)
                    mm.then_inc(hidden_mm, 1)

            def down(e, q, first):
                pe.wait_ge(h_lo_done, e + 1)
                pe.wait_ge(down_lo, e + 1)
                if not first:
                    pe.wait_ge(eout_done, 1 + B * (e - 1))
                for r in range(R // P):
                    out, rows = ps_o[q][:, r * D:(r + 1) * D], slice(r * P, (r + 1) * P)
                    for f in range(KF):
                        pe.matmul(out, h_hi[q][:, f, rows], hi["d"][q][:, f, :], start=f == 0, stop=False)
                        pe.matmul(out, h_hi[q][:, f, rows], lo["d"][q][:, f, :], start=False, stop=False)
                        mm = pe.matmul(out, h_lo[q][:, f, rows], hi["d"][q][:, f, :], start=False, stop=f == KF - 1)
                mm.then_inc(down_mm, 1)

            hidden(0, 0, True)
            hidden(1, 1, True)
            down(0, 0, True)
            with pe.Fori(1, E // 2) as pair:
                hidden(2 * pair, 0, False)
                down(2 * pair - 1, 1, False)
                hidden(2 * pair + 1, 1, False)
                down(2 * pair, 0, False)
            down(E - 1, 1, False)


def combine_stage(nc, c, tag, x_in, x_out, logits_dram, neg_row_max, eout):
    NT = T // P
    W = 2 * D + 2
    LO = D + 2
    BY_POOL = (1, 4, 6)
    BY_DVE = tuple(sc for sc in range(NSC) if sc not in BY_POOL)
    with ExitStack() as ctx:
        al = Scope(nc, ctx, tag)
        lt = [al.sb(f"lt{i}", [P, NSC, GN]) for i in range(2)]
        e_hi = [al.sb(f"e_hi{i}", [P, NSC, GN], F32R) for i in range(2)]
        e_lo = [al.sb(f"e_lo{i}", [P, NSC, GN], F32R) for i in range(2)]
        xin = [al.sb(f"xin{i}", [P, GT, D]) for i in range(2)]
        xout = [al.sb(f"xout{i}", [P, GT, D]) for i in range(2)]
        eo = al.sb("eo", [P, 2, NSC, W], F32R)
        diag = al.sb("diag", [P, GT, P])
        half_inv = [al.sb(f"half_inv{t}", [P, 1]) for t in range(GT)]
        ps_r = [al.ps(f"ps_r{i}", [P, BANK]) for i in range(2)]
        ps_y = [al.ps(f"ps_y{t}", [P, BANK]) for t in range(GT)]
        lt_loaded = [[al.sem(f"lt_loaded{i}{h}") for h in range(2)] for i in range(2)]
        x_loaded = [al.sem(f"x_loaded{i}") for i in range(2)]
        stored = [al.sem(f"stored{i}") for i in range(2)]
        names = ("diag_done", "max_mm", "shifted", "exp_done", "hi_done", "lo_by_dve", "lo_by_pool",
                 "inv_done", "mixed", "finished", "twos_done", "eo_hi_done", "eo_lo_done")
        (diag_done, max_mm, shifted, exp_done, hi_done, lo_by_dve, lo_by_pool,
         inv_done, mixed, finished, twos_done, eo_hi_done, eo_lo_done) = (al.sem(n) for n in names)
        block = ctx.enter_context(nc.Block())
        LAST = B * NG - 1

        def batches(eng, emit):
            emit(0)
            with eng.Fori(1, B - 1) as b:
                emit(b)
            emit(B - 1)

        def exists(b, g, ahead):
            return not isinstance(b, int) or b * NG + g + ahead <= LAST

        def known(b, g):
            return b * NG + g if isinstance(b, int) else B * NG

        @block.sync
        def _(sp):
            x_g = x_in.rearrange("b (g p t) d -> (b g) p t d", g=NG, t=GT)
            y_g = x_out.rearrange("b (g p t) d -> (b g) p t d", g=NG, t=GT)

            def load_logits(n, par):
                for h in range(2):
                    half = slice(h * NSC // 2, (h + 1) * NSC // 2)
                    sp.dma_start(lt[par][:, half, :], logits_dram[n][:, half, :]).then_inc(lt_loaded[par][h], DMA)

            def load_x(n, par):
                sp.dma_start(xin[par][:, :, :], x_g[n]).then_inc(x_loaded[par], DMA)

            def store(n, par):
                sp.wait_ge(finished, GT * (n + 1))
                sp.dma_start(y_g[n], xout[par][:, :, :]).then_inc(stored[par], DMA)

            load_logits(0, 0)
            load_x(0, 0)
            load_logits(1, 1)
            load_x(1, 1)

            def emit(b):
                for g in range(NG):
                    i = b * NG + g
                    if exists(b, g, 2):
                        sp.wait_ge(mixed, GT * i + 1)
                        load_logits(i + 2, g % 2)
                    if known(b, g) >= 1:
                        store(i - 1, (g + 1) % 2)
                        if exists(b, g, 1):
                            load_x(i + 1, (g + 1) % 2)

            batches(sp, emit)
            store(LAST, 1)
            for s in stored:
                sp.wait_ge(s, B * NG // 2 * DMA)

        @block.gpsimd
        def _(pool):
            def max_diagonals(b, g, n):
                if n is not None and (not isinstance(n, int) or n > 0):
                    pool.wait_ge(max_mm, n)
                pool.tensor_tensor(diag[:, :, :], c["ident"][:, :].unsqueeze(1).to_broadcast([P, GT, P]),
                                   neg_row_max[:, b, g, :].unsqueeze(2).to_broadcast([P, GT, P]),
                                   ALU.mult).then_inc(diag_done, 1)

            def lo_part(n, par, sc):
                pool.wait_ge(hi_done, NSC * n + sc + 1)
                pool.tensor_tensor(e_lo[par][:, sc, :], lt[par][:, sc, :], rd(e_hi[par][:, sc, :]),
                                   ALU.subtract).then_inc(lo_by_pool, 1)

            def slot_out_lo(b, par, sc):
                pool.wait_ge(eo_hi_done, NSC * b + sc + 1)
                pool.tensor_tensor(eo[:, par, sc, LO:W], eout[:, b, sc, :], rd(eo[:, par, sc, 0:D]),
                                   ALU.subtract).then_inc(eo_lo_done, 1)

            max_diagonals(0, 0, 0)
            pool.memset(rd(eo[:, :, :, D:LO]), 2.0).then_inc(twos_done, 1)
            max_diagonals(0, 1, 1)
            for sc in BY_POOL:
                lo_part(0, 0, sc)

            def emit(b):
                for g in range(NG):
                    i = b * NG + g
                    if exists(b, g, 2):
                        max_diagonals(b + (g + 2) // NG, (g + 2) % NG, i + 2)
                    for m, sc in enumerate(BY_POOL):
                        if exists(b, g, 1):
                            lo_part(i + 1, (g + 1) % 2, sc)
                        if exists(b, 0, NG) and m < NSC // NG:
                            slot_out_lo(b + 1, (b + 1) % 2, NSC // NG * g + m)

            batches(pool, emit)

        @block.vector
        def _(dve):
            def shift(n, par, sc):
                if sc == 0:
                    dve.wait_ge(max_mm, n + 1)
                if sc % (NSC // 2) == 0:
                    dve.wait_ge(lt_loaded[par][sc // (NSC // 2)], DMA * (n // 2 + 1))
                dve.tensor_tensor(lt[par][:, sc, :], lt[par][:, sc, :], ps_r[par][:, :], ALU.add).then_inc(shifted, 1)

            def lo_part(n, par, sc):
                dve.wait_ge(hi_done, NSC * n + sc + 1)
                dve.tensor_tensor(e_lo[par][:, sc, :], lt[par][:, sc, :], rd(e_hi[par][:, sc, :]),
                                  ALU.subtract).then_inc(lo_by_dve, 1)

            def finish(n, par, t, first):
                dve.wait_ge(mixed, GT * n + t + 1)
                dve.reciprocal(half_inv[t][:, :], ps_y[t][:, D:D + 1]).then_inc(inv_done, 1)
                if t == 0:
                    dve.wait_ge(x_loaded[par], DMA * (n // 2 + 1))
                    if not first:
                        dve.wait_ge(stored[par], DMA * (n // 2))
                dve.wait_ge(inv_done, GT * n + t + 1)
                dve.scalar_tensor_tensor(out=xout[par][:, t, :], in0=ps_y[t][:, 0:D], scalar=half_inv[t][:, :],
                                         in1=xin[par][:, t, :], op0=ALU.mult, op1=ALU.add).then_inc(finished, 1)

            def prepare(n, par, before, done):
                order = ("s0", "s1", "s2", "F3", "l0", "s3", "s4", "s5", "l2", "s6", "f0", "l3", "s7", "f1", "l5", "f2", "l7")
                for what, at in order:
                    if what == "s":
                        shift(n, par, int(at))
                    elif what == "l":
                        lo_part(n, par, int(at))
                    elif what == "F":
                        before()
                    else:
                        done(int(at))

            for sc in range(NSC):
                dve.wait_ge(eo_hi_done, sc + 1)
                dve.tensor_tensor(eo[:, 0, sc, LO:W], eout[:, 0, sc, :], rd(eo[:, 0, sc, 0:D]), ALU.subtract)\
                   .then_inc(eo_lo_done, 1)
            prepare(0, 0, lambda: None, lambda t: None)

            def emit(b):
                for g in range(NG):
                    i = b * NG + g
                    n = known(b, g)
                    before = (lambda: finish(i - 1, (g + 1) % 2, GT - 1, n < 3)) if n >= 1 else (lambda: None)
                    done = lambda t: finish(i, g % 2, t, n < 2)
                    if exists(b, g, 1):
                        prepare(i + 1, (g + 1) % 2, before, done)
                    else:
                        before()
                        for t in range(GT):
                            done(t)

            batches(dve, emit)

        @block.scalar
        def _(act):
            def slot_out_hi(b, par, sc):
                act.activation(eo[:, par, sc, 0:D], eout[:, b, sc, :], ACT.Copy).then_inc(eo_hi_done, 1)

            def exponential(n, par, sc):
                act.wait_ge(shifted, NSC * n + sc + 1)
                act.activation(lt[par][:, sc, :], lt[par][:, sc, :], ACT.Exp).then_inc(exp_done, 1)

            def hi_part(n, par, sc, first):
                if sc == 0 and not first:
                    act.wait_ge(mixed, GT * (n - 1))
                act.wait_ge(exp_done, NSC * n + sc + 1)
                act.activation(e_hi[par][:, sc, :], lt[par][:, sc, :], ACT.Copy).then_inc(hi_done, 1)

            def prepare(n, par, first):
                for sc in range(NSC + 1):
                    if sc < NSC:
                        exponential(n, par, sc)
                    if sc >= 1:
                        hi_part(n, par, sc - 1, first)

            for sc in range(NSC):
                slot_out_hi(0, 0, sc)
            prepare(0, 0, True)

            def emit(b):
                for g in range(NG):
                    i = b * NG + g
                    if exists(b, 0, NG):
                        if g == 0 and known(b, g) > 0:
                            act.wait_ge(mixed, NT * b)
                        for m in range(NSC // NG):
                            slot_out_hi(b + 1, (b + 1) % 2, NSC // NG * g + m)
                    if exists(b, g, 1):
                        prepare(i + 1, (g + 1) % 2, known(b, g) < 1)

            batches(act, emit)

        @block.tensor
        def _(pe):
            def spread_max(n, par, first):
                pe.wait_ge(diag_done, n + 1)
                if not first:
                    pe.wait_ge(shifted, NSC * (n - 1))
                pe.matmul(ps_r[par][:, :], c["ones"][:, :], diag[:, :, :].rearrange("p t q -> p (t q)"),
                          start=True, stop=True).then_inc(max_mm, 1)

            def mix(b, n, par, bpar, t, first):
                if not first:
                    pe.wait_ge(finished, GT * (n - 1) + t + 1)
                tile = slice(t * P, (t + 1) * P)
                for sc in range(NSC + 1):
                    if sc < NSC:
                        if t == 0:
                            pe.wait_ge(hi_done, NSC * n + sc + 1)
                        pe.matmul(ps_y[t][:, 0:LO], e_hi[par][:, sc, tile], eo[:, bpar, sc, 0:LO], start=sc == 0, stop=False)
                        pe.matmul(ps_y[t][:, 0:D], e_hi[par][:, sc, tile], eo[:, bpar, sc, LO:W], start=False, stop=False)
                    sc = sc - 1
                    if sc < 0:
                        continue
                    if t == 0:
                        if sc in BY_POOL:
                            pe.wait_ge(lo_by_pool, len(BY_POOL) * n + BY_POOL.index(sc) + 1)
                        else:
                            pe.wait_ge(lo_by_dve, len(BY_DVE) * n + BY_DVE.index(sc) + 1)
                    mm = pe.matmul(ps_y[t][:, 0:LO], e_lo[par][:, sc, tile], eo[:, bpar, sc, 0:LO],
                                   start=False, stop=sc == NSC - 1)
                mm.then_inc(mixed, 1)

            spread_max(0, 0, True)
            spread_max(1, 1, True)
            pe.wait_ge(twos_done, 1)

            def emit(b):
                for g in range(NG):
                    i = b * NG + g
                    if g == 0:
                        pe.wait_ge(eo_lo_done, NSC * (b + 1))
                    for t in range(GT):
                        mix(b, i, g % 2, b % 2, t, known(b, g) == 0)
                        if t == 0 and exists(b, g, 2):
                            spread_max(i + 2, g % 2, False)

            batches(pe, emit)


def attention_stage(nc, c, tag, prm, x_in, x_out):
    NGR = B * NG
    with ExitStack() as ctx:
        al = Scope(nc, ctx, tag)
        w_raw = {n: al.sb(f"w_{n}", [P, KD, D]) for n in "qkvgo"}
        w_hi = {n: al.sb(f"hi_{n}", [P, KD, D], F32R) for n in "mvgo"}
        w_lo = {n: al.sb(f"lo_{n}", [P, KD, D], F32R) for n in "mvgo"}
        ld, zcol = al.sb("ld", [P, 1]), al.sb("zcol", [P, 6])
        steps, mask = al.sb("steps", [P, P]), al.sb("mask", [P, P])
        xin = [al.sb(f"xin{i}", [P, GT, D]) for i in range(2)]
        xn = [al.sb(f"xn{i}", [P, GT, D]) for i in range(2)]
        base = [al.sb(f"base{i}", [P, GT, D]) for i in range(2)]
        xout = [al.sb(f"xout{i}", [P, GT, D]) for i in range(2)]
        xT_hi = [al.sb(f"xT_hi{i}", [P, KD, GN], F32R) for i in range(2)]
        xT_lo = [al.sb(f"xT_lo{i}", [P, KD, GN], F32R) for i in range(2)]
        xT = [al.sb(f"xT{i}", [P, KD, GN]) for i in range(2)]
        qT, v = al.sb("qT", [P, KD, GN]), al.sb("v", [P, GT, D])
        gate = [al.sb(f"gate{i}", [P, KD, GN]) for i in range(2)]
        sc = al.sb("sc", [P, GT, P])
        o, o_hi, o_lo = al.sb("o", [P, KD, GN]), al.sb("o_hi", [P, KD, GN], F32R), al.sb("o_lo", [P, KD, GN], F32R)
        stats, mv = al.sb("stats", [P, GT, 6]), [al.sb(f"mv{i}", [P, GT, 2]) for i in range(2)]
        var_eps, rstd = al.sb("var_eps", [P, GT]), [al.sb(f"rstd{i}", [P, GT]) for i in range(2)]
        ps = [al.ps(f"ps{i}", [P, BANK]) for i in range(8)]
        ps_t, ps_q, ps_v, ps_g = ps[0:2], ps[2:4], ps[4:6], ps[6:8]

        def weights_block():
            with ExitStack() as wctx:
                wa = Scope(nc, wctx, tag + "w_")
                loaded, w_tr, hi_done, lo_done = (wa.sem(n) for n in ("loaded", "w_tr", "hi_done", "lo_done"))
                z_step, a_step, steps_done, mask_done = (wa.sem(n) for n in ("z_step", "a_step", "steps_done", "mask_done"))
                block = wctx.enter_context(nc.Block())
                jobs = [(n, k) for n in "mvgo" for k in range(KD)]

                @block.sync
                def _(sp):
                    for n in "qkvgo":
                        sp.dma_start(w_raw[n][:, :, :], prm["W_" + n].rearrange("(k p) d -> p k d", p=P)).then_inc(loaded, DMA)
                    sp.dma_start(ld[:, :], prm["log_decay"][0:1].rearrange("(a n) -> a n", a=1).to_broadcast([P, 1]))                      .then_inc(loaded, DMA)
                    sp.wait_ge(loaded, 6 * DMA)

                @block.gpsimd
                def _(pool):
                    pool.iota(steps[:, :], [[1, P]], base=0, channel_multiplier=-1,
                              allow_small_or_imprecise_dtypes=True).then_inc(steps_done, 1)
                    pool.wait_ge(a_step, 3)
                    blocks = mask[:, :].rearrange("p (c i) -> p c i", i=CHUNK)
                    pool.affine_select(out=mask[:, :], in_=mask[:, :], compare_op=ALU.is_ge, fill=0.0, base=0,
                                       pattern=[[1, P]], channel_multiplier=-1).then_inc(mask_done, 1)
                    pool.wait_ge(mask_done, 1)
                    pool.affine_select(out=blocks, in_=blocks, compare_op=ALU.is_ge, fill=0.0, base=0,
                                       pattern=[[-CHUNK, P // CHUNK], [0, CHUNK]], channel_multiplier=1).then_inc(mask_done, 1)

                @block.scalar
                def _(act):
                    act.wait_ge(z_step, 2)
                    act.activation(zcol[:, 2:3], zcol[:, 1:2], ACT.Exp, scale=-1.0).then_inc(a_step, 1)
                    act.wait_ge(a_step, 1)
                    act.activation(zcol[:, 3:4], zcol[:, 2:3], ACT.Ln, bias=c["ones"][:, 0:1]).then_inc(a_step, 1)
                    act.wait_ge(z_step, 5)
                    act.activation(mask[:, :], steps[:, :], ACT.Exp, scale=zcol[:, 4:5]).then_inc(a_step, 1)
                    for n, (w, k) in enumerate(jobs):
                        act.wait_ge(w_tr, n + 1)
                        act.activation(w_hi[w][:, k, :], ps[n][:, 0:D], ACT.Copy).then_inc(hi_done, 1)

                @block.vector
                def _(dve):
                    dve.wait_ge(loaded, 6 * DMA)
                    dve.tensor_scalar(zcol[:, 0:1], ld[:, :], -1.0, 0.0, ALU.mult, ALU.max).then_inc(z_step, 1)
                    dve.wait_ge(z_step, 1)
                    dve.scalar_tensor_tensor(out=zcol[:, 1:2], in0=zcol[:, 0:1], scalar=2.0, in1=ld[:, :],
                                             op0=ALU.mult, op1=ALU.add).then_inc(z_step, 1)
                    dve.wait_ge(a_step, 2)
                    dve.tensor_tensor(zcol[:, 5:6], zcol[:, 0:1], zcol[:, 3:4], ALU.add).then_inc(z_step, 1)
                    dve.wait_ge(z_step, 3)
                    dve.tensor_scalar(zcol[:, 4:5], zcol[:, 5:6], -1.0, None, ALU.mult).then_inc(z_step, 1)
                    dve.wait_ge(steps_done, 1)
                    dve.tensor_scalar(steps[:, :], steps[:, :], 0.0, None, ALU.max).then_inc(z_step, 1)
                    for n, (w, k) in enumerate(jobs):
                        dve.wait_ge(hi_done, n + 1)
                        dve.tensor_tensor(w_lo[w][:, k, :], ps[n][:, 0:D], rd(w_hi[w][:, k, :]), ALU.subtract).then_inc(lo_done, 1)

                @block.tensor
                def _(pe):
                    pe.wait_ge(loaded, 6 * DMA)
                    for n, (w, k) in enumerate(jobs):
                        cols = slice(k * P, (k + 1) * P)
                        for j in range(KD):
                            if w == "m":
                                mm = pe.matmul(ps[n][:, 0:D], w_raw["q"][:, j, cols], w_raw["k"][:, j, :],
                                               start=j == 0, stop=j == KD - 1)
                            else:
                                mm = pe.transpose(ps[n][:, j * P:(j + 1) * P], w_raw[w][:, j, cols], c["ident"][:, :])
                        mm.then_inc(w_tr, 1)

        weights_block()
        x_loaded = [al.sem(f"x_loaded{i}") for i in range(2)]
        stored = [al.sem(f"stored{i}") for i in range(2)]
        names = ("stats_done", "mv_done", "var_done", "rstd_done", "xn_done", "base_done", "xT_tr", "xT_hi_done",
                 "xT_lo_done", "xT_out", "q_mm", "q_out", "gate_mm", "gate_done", "v_mm", "v_out",
                 "s_mm", "s_masked", "o_mm", "o_gated", "o_hi_done", "o_lo_done", "y_mm", "y_done")
        (stats_done, mv_done, var_done, rstd_done, xn_done, base_done, xT_tr, xT_hi_done,
         xT_lo_done, xT_out, q_mm, q_out, gate_mm, gate_done, v_mm, v_out,
         s_mm, s_masked, o_mm, o_gated, o_hi_done, o_lo_done, y_mm, y_done) = (al.sem(n) for n in names)
        block = ctx.enter_context(nc.Block())

        def groups(eng, emit):
            emit(0, 0, False, 2)
            emit(1, 1, True, 2)
            with eng.Fori(1, NGR // 2 - 1) as pair:
                for q in range(2):
                    emit(2 * pair + q, q, True, 2)
            emit(NGR - 2, 0, True, 1)
            emit(NGR - 1, 1, True, 0)

        @block.sync
        def _(sp):
            x_g = x_in.rearrange("b (g t p) d -> (b g) p t d", g=NG, t=GT)
            y_g = x_out.rearrange("b (g t p) d -> (b g) p t d", g=NG, t=GT)
            for n in range(2):
                sp.dma_start(xin[n][:, :, :], x_g[n]).then_inc(x_loaded[n], DMA)

            def emit(g, q, before, ahead):
                if ahead == 2:
                    sp.wait_ge(base_done, g + 1)
                    sp.dma_start(xin[q][:, :, :], x_g[g + 2]).then_inc(x_loaded[q], DMA)
                if before:
                    sp.wait_ge(y_done, KD * g)
                    sp.dma_start(y_g[g - 1], xout[1 - q][:, :, :]).then_inc(stored[1 - q], DMA)

            groups(sp, emit)
            sp.wait_ge(y_done, KD * NGR)
            sp.dma_start(y_g[NGR - 1], xout[1][:, :, :]).then_inc(stored[1], DMA)
            for s in stored:
                sp.wait_ge(s, 1 + NGR // 2 * DMA)

        @block.gpsimd
        def _(pool):
            def norm_scale(g, q):
                pool_wait(pool, c, mv_done, GT * (g + 1))
                pool.tensor_scalar(var_eps[:, :], mv[q][:, :, 1], 1.0, EPS, ALU.mult, ALU.add).then_inc(var_done, 1)
                pool.wait_ge(var_done, g + 1)
                pool.tensor_tensor(rstd[q][:, :], var_eps[:, :], c["minus_half"][:, 0:GT], ALU.pow).then_inc(rstd_done, 1)

            def residual(g, q, first):
                pool.wait_ge(xn_done, g + 1)
                if not first:
                    pool.wait_ge(y_done, KD * (g - 1))
                pool.tensor_tensor(base[q][:, :, :], xin[q][:, :, :], xn[q][:, :, :], ALU.add).then_inc(base_done, 1)

            norm_scale(0, 0)
            residual(0, 0, True)

            def emit(g, q, before, ahead):
                if ahead >= 1:
                    norm_scale(g + 1, 1 - q)
                    residual(g + 1, 1 - q, not before)

            groups(pool, emit)

        @block.vector
        def _(dve):
            def token_stats(g, q):
                dve.wait_ge(x_loaded[q], DMA * (g // 2 + 1))
                for t in range(GT):
                    dve.bn_stats(stats[:, t, :], xin[q][:, t, :]).then_inc(stats_done, 1)
                dve_wait(dve, c, stats_done, GT * (g + 1))
                for t in range(GT):
                    dve.bn_aggr(mv[q][:, t, :], stats[:, t, :]).then_inc(mv_done, 1)

            def normalize(g, q, first):
                dve.wait_ge(rstd_done, g + 1)
                dve.wait_ge(mv_done, GT * (g + 1))
                if not first:
                    dve.wait_ge(xT_tr, KD * (g - 1))
                    dve.wait_ge(base_done, g - 1)
                for t in range(GT):
                    last = dve.tensor_scalar(xn[q][:, t, :], xin[q][:, t, :], mv[q][:, t, 0:1],
                                             rstd[q][:, t:t + 1], ALU.subtract, ALU.mult)
                last.then_inc(xn_done, 1)

            def minus_hi(lo, src, hi, ready, count, done):
                dve.wait_ge(ready, count)
                dve.tensor_tensor(lo, src, rd(hi), ALU.subtract).then_inc(done, 1)

            def tokens_lo(g, q):
                for k in range(KD):
                    minus_hi(xT_lo[q][:, k, :], xT[q][:, k, :], xT_hi[q][:, k, :], xT_hi_done, KD * g + k + 1, xT_lo_done)

            def scores(g):
                dve.wait_ge(s_mm, g + 1)
                dve.tensor_tensor(sc[:, :, :], ps_g[0][:, :].rearrange("p (t n) -> p t n", n=P),
                                  mask[:, :].unsqueeze(1).to_broadcast([P, GT, P]), ALU.mult).then_inc(s_masked, 1)

            def gated(g, q):
                dve.wait_ge(gate_done, KD * (g + 1))
                for k in range(KD):
                    dve.wait_ge(o_mm, KD * g + k + 1)
                    dve.tensor_tensor(o[:, k, :], ps_v[k][:, :], gate[q][:, k, :], ALU.mult).then_inc(o_gated, 1)

            def gated_lo(g):
                for k in range(KD):
                    minus_hi(o_lo[:, k, :], o[:, k, :], o_hi[:, k, :], o_hi_done, KD * g + k + 1, o_lo_done)

            def finish(g, q, first):
                dve.wait_ge(base_done, g + 1)
                if not first:
                    dve.wait_ge(stored[q], 1 + DMA * (g // 2))
                for h in range(KD):
                    dve.wait_ge(y_mm, KD * g + h + 1)
                    dve.tensor_tensor(xout[q][:, 2 * h:2 * h + 2, :], ps_t[h][:, :].rearrange("p (t d) -> p t d", d=D),
                                      base[q][:, 2 * h:2 * h + 2, :], ALU.add).then_inc(y_done, 1)

            for s in stored:
                dve.sem_inc(s, 1)
            token_stats(0, 0)
            normalize(0, 0, True)
            tokens_lo(0, 0)

            def emit(g, q, before, ahead):
                if ahead >= 1:
                    token_stats(g + 1, 1 - q)
                if ahead >= 1:
                    normalize(g + 1, 1 - q, not before)
                if before:
                    gated(g - 1, 1 - q)
                    gated_lo(g - 1)
                if ahead >= 1:
                    tokens_lo(g + 1, 1 - q)
                if before:
                    finish(g - 1, 1 - q, isinstance(g, int) and g <= 2)
                scores(g)

            groups(dve, emit)
            gated(NGR - 1, 1)
            gated_lo(NGR - 1)
            finish(NGR - 1, 1, False)

        @block.scalar
        def _(act):
            def tokens_hi(g, q):
                for k in range(KD):
                    act.wait_ge(xT_tr, KD * g + k + 1)
                    act.activation(xT[q][:, k, :], ps_t[k][:, :], ACT.Copy).then_inc(xT_out, 1)
                for k in range(KD):
                    act.wait_ge(xT_out, KD * g + k + 1)
                    act.activation(xT_hi[q][:, k, :], xT[q][:, k, :], ACT.Copy).then_inc(xT_hi_done, 1)

            def gated_hi(g):
                for k in range(KD):
                    act.wait_ge(o_gated, KD * g + k + 1)
                    act.activation(o_hi[:, k, :], o[:, k, :], ACT.Copy).then_inc(o_hi_done, 1)

            tokens_hi(0, 0)

            def emit(g, q, before, ahead):
                for k in range(KD):
                    act.wait_ge(q_mm, KD * g + k + 1)
                    act.activation(qT[:, k, :], ps_q[k][:, :], ACT.Copy).then_inc(q_out, 1)
                if before:
                    gated_hi(g - 1)
                for k in range(KD):
                    act.wait_ge(gate_mm, KD * g + k + 1)
                    act.activation(gate[q][:, k, :], ps_g[k][:, :], ACT.Sigmoid).then_inc(gate_done, 1)
                if ahead >= 1:
                    tokens_hi(g + 1, 1 - q)
                for h in range(KD):
                    act.wait_ge(v_mm, KD * g + h + 1)
                    act.activation(v[:, 2 * h:2 * h + 2, :], ps_v[h][:, :].rearrange("p (t d) -> p t d", d=D),
                                   ACT.Copy).then_inc(v_out, 1)

            groups(act, emit)
            gated_hi(NGR - 1)

        @block.tensor
        def _(pe):
            def three(out, a_hi, a_lo, b_hi, b_lo, start, stop):
                pe.matmul(out, a_hi, b_hi, start=start, stop=False)
                pe.matmul(out, a_hi, b_lo, start=False, stop=False)
                return pe.matmul(out, a_lo, b_hi, start=False, stop=stop)

            def transpose_tokens(g, q):
                pe.wait_ge(xn_done, g + 1)
                for k in range(KD):
                    for t in range(GT):
                        mm = pe.transpose(ps_t[k][:, t * P:(t + 1) * P], xn[q][:, t, k * P:(k + 1) * P], c["ident"][:, :])
                    mm.then_inc(xT_tr, 1)

            def project(banks, w, q, done):
                for m in range(KD):
                    cols = slice(m * P, (m + 1) * P)
                    for k in range(KD):
                        mm = three(banks[m][:, :], w_hi[w][:, k, cols], w_lo[w][:, k, cols],
                                   xT_hi[q][:, k, :], xT_lo[q][:, k, :], k == 0, k == KD - 1)
                    mm.then_inc(done, 1)

            def rows(banks, a_hi, a_lo, w, done):
                for t in range(GT):
                    out = banks[t // 2][:, (t % 2) * D:(t % 2 + 1) * D]
                    for k in range(KD):
                        mm = three(out, a_hi[:, k, t * P:(t + 1) * P], a_lo[:, k, t * P:(t + 1) * P],
                                   w_hi[w][:, k, :], w_lo[w][:, k, :], k == 0, k == KD - 1)
                    if t % 2:
                        mm.then_inc(done, 1)

            def mix_values(g):
                pe.wait_ge(s_masked, g + 1)
                pe.wait_ge(v_out, KD * (g + 1))
                for k in range(KD):
                    cols = slice(k * P, (k + 1) * P)
                    for t in range(GT):
                        mm = pe.matmul(ps_v[k][:, t * P:(t + 1) * P], v[:, t, cols], sc[:, t, :], start=True, stop=True)
                    mm.then_inc(o_mm, 1)

            transpose_tokens(0, 0)

            def emit(g, q, before, ahead):
                pe.wait_ge(xT_lo_done, KD * (g + 1))
                pe.wait_ge(q_out, KD * g)
                project(ps_q, "m", q, q_mm)
                if before:
                    mix_values(g - 1)
                    pe.wait_ge(s_masked, g)
                project(ps_g, "g", q, gate_mm)
                if ahead >= 1:
                    if before:
                        if not (isinstance(g, int) and g == 1):
                            pe.wait_ge(y_done, KD * (g - 1))
                    pe.wait_ge(xT_out, KD * (g + 1))
                    transpose_tokens(g + 1, 1 - q)
                if before:
                    pe.wait_ge(o_gated, KD * g)
                rows(ps_v, xT_hi[q], xT_lo[q], "v", v_mm)
                if before:
                    pe.wait_ge(o_lo_done, KD * g)
                    if ahead >= 1:
                        pe.wait_ge(xT_out, KD * (g + 2))
                    rows(ps_t, o_hi, o_lo, "o", y_mm)
                pe.wait_ge(gate_done, KD * (g + 1))
                pe.wait_ge(q_out, KD * (g + 1))
                pe.wait_ge(xT_out, KD * (g + 1))
                for t in range(GT):
                    cols = slice(t * P, (t + 1) * P)
                    for k in range(KD):
                        mm = pe.matmul(ps_g[0][:, cols], xT[q][:, k, cols], qT[:, k, cols],
                                       start=k == 0, stop=k == KD - 1)
                mm.then_inc(s_mm, 1)

            groups(pe, emit)
            mix_values(NGR - 1)
            pe.wait_ge(o_lo_done, KD * NGR)
            pe.wait_ge(y_done, KD * (NGR - 1))
            rows(ps_t, o_hi, o_lo, "o", y_mm)


def feed_forward(nc, c, tag, prm, x_in, x_out, scratch):
    with ExitStack() as ctx:
        neg_row_max = ctx.enter_context(nc.sbuf_tensor(tag + "neg_row_max", [P, B, NG, GT], F32))
        with nc.sbuf_tensor(tag + "slots", [P, KD, E, B, S], F32) as slots:
            route_stage(nc, c, tag + "r_", x_in, slots, neg_row_max, scratch["logits"], scratch["normalized"])
            eout = ctx.enter_context(nc.sbuf_tensor(tag + "eout", [P, B, NSC, D], F32, side="right"))
            expert_stage(nc, c, tag + "e_", prm, slots, eout)
        combine_stage(nc, c, tag + "c_", x_in, x_out, scratch["logits"], neg_row_max, eout)


def macaron_kernel(nc, prm, out):
    with ExitStack() as ctx:
        al = Scope(nc, ctx, "")
        c = {n: al.sb(n, [P, w]) for n, w in (("ident", P), ("ones", P), ("minus_half", 8), ("dve_carrier", 1), ("pool_carrier", 2),
                                              ("gain", KD), ("shift", KD), ("slot_shift", NSC),
                                              ("biases", 2 * E * KF))}
        c["emb_hi"], c["emb_lo"] = al.sb("emb_hi", [P, KD, SL], F32R), al.sb("emb_lo", [P, KD, SL], F32R)
        scratch = {"logits": nc.dram_tensor("logits", (B * NG, P, NSC, GN), F32, kind="Internal").ap(),
                   "normalized": nc.dram_tensor("normalized", (B * NG, P, GT, D), F32, kind="Internal").ap()}
        x_a = nc.dram_tensor("x_after_ffn", (B, T, D), F32, kind="Internal").ap()
        x_b = nc.dram_tensor("x_after_attention", (B, T, D), F32, kind="Internal").ap()
        setup_stage(nc, c, prm)
        feed_forward(nc, c, "f1", prm, prm["x"], x_a, scratch)
        attention_stage(nc, c, "at_", prm, x_a, x_b)
        feed_forward(nc, c, "f2", prm, x_b, out, scratch)


_INS = {"x": "L0_attn_x", "W_q": "L0_attn_W_q", "W_k": "L0_attn_W_k", "W_v": "L0_attn_W_v", "W_g": "L0_attn_W_g",
        "W_o": "L0_attn_W_o", "log_decay": "L0_attn_log_decay", "norm_g": "L0_ffn_norm_g", "norm_b": "L0_ffn_norm_b",
        "slot_g": "L0_ffn_slot_g", "slot_b": "L0_ffn_slot_b", "scale": "L0_ffn_scale",
        "slot_embeds": "L0_ffn_slot_embeds", "Wg": "L0_ffn_Wg", "bg": "L0_ffn_bg", "Wu": "L0_ffn_Wu",
        "bu": "L0_ffn_bu", "Wd": "L0_ffn_Wd", "bd": "L0_ffn_bd"}


def kernel(**inputs):
    import numpy as _np
    import concourse.bacc as _bacc
    from concourse import mybir as _mybir
    from concourse.bass_utils import run_bass_kernel_spmd as _run

    nc = _bacc.Bacc("TRN2", target_bir_lowering=False, num_devices=1)
    arrays, prm = {}, {}
    for short, name in _INS.items():
        a = _np.ascontiguousarray(inputs[name])
        arrays[f"in_{name}"] = a
        prm[short] = nc.dram_tensor(f"in_{name}", a.shape, _mybir.dt.from_np(a.dtype), kind="ExternalInput").ap()
    out = nc.dram_tensor("out", (B, T, D), _mybir.dt.float32, kind="ExternalOutput").ap()
    macaron_kernel(nc, prm, out)
    r = _run(nc, [arrays], core_ids=[0])
    return r.results[0]["out"]
```
